# Optimizing a Trainium2 kernel written in Bass

```python
import numpy as np
import jax
import jax.numpy as jnp

def _softmax(x, axis=-1):
    return jax.nn.softmax(x, axis=axis)

def _gelu(x):
    return jax.nn.gelu(x, approximate=True)

def _silu(x):
    return jax.nn.silu(x)

def _sigmoid(x):
    return jax.nn.sigmoid(x)

def _layernorm(x, axis=-1, eps=1e-05):
    m = jnp.mean(x, axis=axis, keepdims=True)
    v = jnp.var(x, axis=axis, keepdims=True)
    return (x - m) / jnp.sqrt(v + eps)

def _scatter_add(tgt, idx, src, axis=0):
    return tgt.at[idx].add(src)

def _segment_sum(src, seg, n):
    return jax.ops.segment_sum(src, seg, n)
kernel_name = 'mk_vit_tower_postln_d1_tok_img768_r4_80e2cc'

def setup_inputs(seed: int=0):
    np.random.seed(seed)
    _w = jnp.asarray

    def _rec_inputs():
        import jax
        import jax.numpy as jnp
        _rk = jax.random.key(seed)
        x = -0.000222058 + 0.999998 * jax.random.normal(jax.random.fold_in(_rk, 1), (32, 3, 96, 96), jnp.float32)
        return x
    x = _rec_inputs()

    def _L0_tok_setup():
        import jax, jax.numpy as jnp
        import numpy as np
        KERNEL = 16
        C = 3
        H = 128
        B = 32
        IN_FEAT = C * KERNEL * KERNEL
        HIDDEN = 192
        key = jax.random.key(seed)
        k1, k2, k3 = jax.random.split(key, 3)
        x = jax.random.normal(k1, (B, C, H, H), dtype=jnp.float32)
        bound = float(np.sqrt(6.0 / IN_FEAT))
        W = jax.random.uniform(k2, (HIDDEN, IN_FEAT), dtype=jnp.float32, minval=-bound, maxval=bound)
        b = jnp.zeros((HIDDEN,), dtype=jnp.float32)
        return {'x': x, 'W': W, 'b': b}
    _L0_tok_all = _L0_tok_setup()
    _L0_tok_in = {k: v for k, v in _L0_tok_all.items() if k in ('W', 'b')}
    del _L0_tok_all

    def _L0_attn_setup():
        import jax, jax.numpy as jnp
        import numpy as np
        NB_REF = 10
        HEADS = 12
        STEPS = 3
        TAU = 0.5
        LN_EPS = 1e-05
        COS_EPS = 1e-08

        def _encoder(z, fc1_w, fc1_b, fc2_w, fc2_b):
            h = jax.nn.gelu(z @ fc1_w + fc1_b, approximate=False)
            return h @ fc2_w + fc2_b

        def _layernorm(z, g, b):
            mu = jnp.mean(z, axis=-1, keepdims=True)
            var = jnp.mean(jnp.square(z - mu), axis=-1, keepdims=True)
            return (z - mu) * jax.lax.rsqrt(var + LN_EPS) * g + b

        def _projector_mask(x, ref, fc1_w, fc1_b, fc2_w, fc2_b):
            ex = _encoder(x, fc1_w, fc1_b, fc2_w, fc2_b)
            er = _encoder(ref, fc1_w, fc1_b, fc2_w, fc2_b)
            nx = jnp.maximum(jnp.linalg.norm(ex, axis=-1), COS_EPS)
            nr = jnp.maximum(jnp.linalg.norm(er, axis=-1), COS_EPS)
            cos = jnp.einsum('bne,rne->bnr', ex, er) / (nx[:, :, None] * nr.T[None])
            c = (jnp.mean(cos, axis=2) + 1.0) / 2.0
            return (0.5 + 0.5 * jnp.tanh(25.0 * (c - TAU)))[:, :, None]

        def _diffuser(x, ref, qv_w, k_w, proj_w, proj_b, ln_g, ln_b):
            B, N, C = x.shape
            hd = C // HEADS
            scale = hd ** (-0.5)
            k = (ref @ k_w).reshape(NB_REF, N, HEADS, hd).transpose(0, 2, 1, 3)
            for _ in range(STEPS):
                qv = (x @ qv_w).reshape(B, N, 2, HEADS, hd).transpose(2, 0, 3, 1, 4)
                q, v = (qv[0], qv[1])
                attn = jnp.einsum('bhnd,rhmd->brhnm', q, k) * scale
                attn = jnp.einsum('brhnm,brhkm->brhnk', attn, attn)
                o = jnp.einsum('brhnk,bhkd->brhnd', attn, v)
                o = o.reshape(B, NB_REF, N, C)
                x = jnp.mean(o.transpose(0, 2, 3, 1), axis=-1)
                x = _layernorm(x @ proj_w + proj_b, ln_g, ln_b)
            return x
        key = jax.random.key(seed)
        ks = jax.random.split(key, 11)
        D, B, N = (192, 8, 197)
        s = 0.02
        return {'x': jax.random.normal(ks[0], (B + NB_REF, N, D), jnp.float32), 'qv_w': jax.random.normal(ks[1], (D, 2 * D), jnp.float32) * s, 'k_w': jax.random.normal(ks[2], (D, D), jnp.float32) * s, 'proj_w': jax.random.normal(ks[3], (D, D), jnp.float32) * s, 'proj_b': jnp.zeros((D,), jnp.float32), 'ln_g': jnp.ones((D,), jnp.float32), 'ln_b': jnp.zeros((D,), jnp.float32), 'fc1_w': jax.random.normal(ks[4], (D, D // 4), jnp.float32) * s, 'fc1_b': jnp.zeros((D // 4,), jnp.float32), 'fc2_w': jax.random.normal(ks[5], (D // 4, D // 8), jnp.float32) * s, 'fc2_b': jnp.zeros((D // 8,), jnp.float32)}
    _L0_attn_all = _L0_attn_setup()
    _L0_attn_in = {k: v for k, v in _L0_attn_all.items() if k in ('qv_w', 'k_w', 'proj_w', 'proj_b', 'ln_g', 'ln_b', 'fc1_w', 'fc1_b', 'fc2_w', 'fc2_b')}
    del _L0_attn_all

    def _L0_ffn_setup():
        import jax, jax.numpy as jnp
        import numpy as np
        DIM = 192
        HEADS = 12
        EXPERTS = 8
        HID = 768
        TOP_K = 2
        LN_EPS = 1e-05

        def _layer_norm(x, g, b):
            mu = x.mean(-1, keepdims=True)
            var = ((x - mu) ** 2).mean(-1, keepdims=True)
            return (x - mu) * jax.lax.rsqrt(var + LN_EPS) * g + b

        def _attention(x, qkv_w, qkv_b, proj_w, proj_b):
            B, N, C = x.shape
            hd = C // HEADS
            qkv = (x @ qkv_w + qkv_b).reshape(B, N, 3, HEADS, hd).transpose(2, 0, 3, 1, 4)
            q, k, v = (qkv[0], qkv[1], qkv[2])
            attn = jax.nn.softmax(jnp.einsum('bhnd,bhmd->bhnm', q, k) * hd ** (-0.5), axis=-1)
            o = jnp.einsum('bhnm,bhmd->bhnd', attn, v).transpose(0, 2, 1, 3).reshape(B, N, C)
            return o @ proj_w + proj_b

        def _moe_mlp(xn, gate_w, w1, b1, w2, b2):
            T = xn.shape[0]
            logits = xn @ gate_w
            top_logits, top_idx = jax.lax.top_k(logits, TOP_K)
            top_gates = jax.nn.softmax(top_logits, axis=-1)
            gates = jnp.zeros((T, EXPERTS), xn.dtype).at[jnp.arange(T)[:, None], top_idx].set(top_gates)
            h = jax.nn.gelu(jnp.einsum('td,edh->teh', xn, w1) + b1, approximate=False)
            y = jnp.einsum('teh,ehd->ted', h, w2) + b2
            return jnp.einsum('ted,te->td', y, gates)
        key = jax.random.key(seed)
        ks = jax.random.split(key, 16)
        s = 0.02
        return {'x': jax.random.normal(ks[0], (8, 196, DIM), jnp.float32), 'ln1_g': jnp.ones((DIM,), jnp.float32), 'ln1_b': jnp.zeros((DIM,), jnp.float32), 'qkv_w': jax.random.normal(ks[1], (DIM, 3 * DIM), jnp.float32) * s, 'qkv_b': jnp.zeros((3 * DIM,), jnp.float32), 'proj_w': jax.random.normal(ks[2], (DIM, DIM), jnp.float32) * s, 'proj_b': jnp.zeros((DIM,), jnp.float32), 'ln2_g': jnp.ones((DIM,), jnp.float32), 'ln2_b': jnp.zeros((DIM,), jnp.float32), 'gate_w': jax.random.normal(ks[3], (DIM, EXPERTS), jnp.float32) * s, 'w1': jax.random.normal(ks[4], (EXPERTS, DIM, HID), jnp.float32) * s, 'b1': jnp.zeros((EXPERTS, HID), jnp.float32), 'w2': jax.random.normal(ks[5], (EXPERTS, HID, DIM), jnp.float32) * s, 'b2': jnp.zeros((EXPERTS, DIM), jnp.float32)}
    _L0_ffn_all = _L0_ffn_setup()
    _L0_ffn_in = {k: v for k, v in _L0_ffn_all.items() if k in ('ln1_g', 'ln1_b', 'qkv_w', 'qkv_b', 'proj_w', 'proj_b', 'ln2_g', 'ln2_b', 'gate_w', 'w1', 'b1', 'w2', 'b2')}
    del _L0_ffn_all
    return {'x': x, 'L0_tok_W': _L0_tok_in['W'], 'L0_tok_b': _L0_tok_in['b'], 'L0_attn_qv_w': _L0_attn_in['qv_w'], 'L0_attn_k_w': _L0_attn_in['k_w'], 'L0_attn_proj_w': _L0_attn_in['proj_w'], 'L0_attn_proj_b': _L0_attn_in['proj_b'], 'L0_attn_ln_g': _L0_attn_in['ln_g'], 'L0_attn_ln_b': _L0_attn_in['ln_b'], 'L0_attn_fc1_w': _L0_attn_in['fc1_w'], 'L0_attn_fc1_b': _L0_attn_in['fc1_b'], 'L0_attn_fc2_w': _L0_attn_in['fc2_w'], 'L0_attn_fc2_b': _L0_attn_in['fc2_b'], 'L0_ffn_ln1_g': _L0_ffn_in['ln1_g'], 'L0_ffn_ln1_b': _L0_ffn_in['ln1_b'], 'L0_ffn_qkv_w': _L0_ffn_in['qkv_w'], 'L0_ffn_qkv_b': _L0_ffn_in['qkv_b'], 'L0_ffn_proj_w': _L0_ffn_in['proj_w'], 'L0_ffn_proj_b': _L0_ffn_in['proj_b'], 'L0_ffn_ln2_g': _L0_ffn_in['ln2_g'], 'L0_ffn_ln2_b': _L0_ffn_in['ln2_b'], 'L0_ffn_gate_w': _L0_ffn_in['gate_w'], 'L0_ffn_w1': _L0_ffn_in['w1'], 'L0_ffn_b1': _L0_ffn_in['b1'], 'L0_ffn_w2': _L0_ffn_in['w2'], 'L0_ffn_b2': _L0_ffn_in['b2']}

def reference(x, L0_tok_W, L0_tok_b, L0_attn_qv_w, L0_attn_k_w, L0_attn_proj_w, L0_attn_proj_b, L0_attn_ln_g, L0_attn_ln_b, L0_attn_fc1_w, L0_attn_fc1_b, L0_attn_fc2_w, L0_attn_fc2_b, L0_ffn_ln1_g, L0_ffn_ln1_b, L0_ffn_qkv_w, L0_ffn_qkv_b, L0_ffn_proj_w, L0_ffn_proj_b, L0_ffn_ln2_g, L0_ffn_ln2_b, L0_ffn_gate_w, L0_ffn_w1, L0_ffn_b1, L0_ffn_w2, L0_ffn_b2):
    import jax
    import jax.numpy as jnp

    def _L0_tok_ref(x, W, b):
        import jax, jax.numpy as jnp
        import numpy as np
        KERNEL = 16
        C = 3
        H = 128
        B = 32
        IN_FEAT = C * KERNEL * KERNEL
        HIDDEN = 192
        bsz, c, h, w = x.shape
        step = h // KERNEL
        p = x.reshape(bsz, c, step, KERNEL, step, KERNEL)
        p = p.transpose(0, 2, 4, 1, 3, 5)
        p = p.reshape(bsz, step * step, c * KERNEL * KERNEL)
        return jnp.einsum('blf,hf->blh', p, W) + b

    def _L0_attn_ref(x, qv_w, k_w, proj_w, proj_b, ln_g, ln_b, fc1_w, fc1_b, fc2_w, fc2_b):
        import jax, jax.numpy as jnp
        import numpy as np
        NB_REF = 10
        HEADS = 12
        STEPS = 3
        TAU = 0.5
        LN_EPS = 1e-05
        COS_EPS = 1e-08

        def _encoder(z, fc1_w, fc1_b, fc2_w, fc2_b):
            h = jax.nn.gelu(z @ fc1_w + fc1_b, approximate=False)
            return h @ fc2_w + fc2_b

        def _layernorm(z, g, b):
            mu = jnp.mean(z, axis=-1, keepdims=True)
            var = jnp.mean(jnp.square(z - mu), axis=-1, keepdims=True)
            return (z - mu) * jax.lax.rsqrt(var + LN_EPS) * g + b

        def _projector_mask(x, ref, fc1_w, fc1_b, fc2_w, fc2_b):
            ex = _encoder(x, fc1_w, fc1_b, fc2_w, fc2_b)
            er = _encoder(ref, fc1_w, fc1_b, fc2_w, fc2_b)
            nx = jnp.maximum(jnp.linalg.norm(ex, axis=-1), COS_EPS)
            nr = jnp.maximum(jnp.linalg.norm(er, axis=-1), COS_EPS)
            cos = jnp.einsum('bne,rne->bnr', ex, er) / (nx[:, :, None] * nr.T[None])
            c = (jnp.mean(cos, axis=2) + 1.0) / 2.0
            return (0.5 + 0.5 * jnp.tanh(25.0 * (c - TAU)))[:, :, None]

        def _diffuser(x, ref, qv_w, k_w, proj_w, proj_b, ln_g, ln_b):
            B, N, C = x.shape
            hd = C // HEADS
            scale = hd ** (-0.5)
            k = (ref @ k_w).reshape(NB_REF, N, HEADS, hd).transpose(0, 2, 1, 3)
            for _ in range(STEPS):
                qv = (x @ qv_w).reshape(B, N, 2, HEADS, hd).transpose(2, 0, 3, 1, 4)
                q, v = (qv[0], qv[1])
                attn = jnp.einsum('bhnd,rhmd->brhnm', q, k) * scale
                attn = jnp.einsum('brhnm,brhkm->brhnk', attn, attn)
                o = jnp.einsum('brhnk,bhkd->brhnd', attn, v)
                o = o.reshape(B, NB_REF, N, C)
                x = jnp.mean(o.transpose(0, 2, 3, 1), axis=-1)
                x = _layernorm(x @ proj_w + proj_b, ln_g, ln_b)
            return x
        xm, ref = (x[:-NB_REF], jax.lax.stop_gradient(x[-NB_REF:]))
        correct_m = _projector_mask(xm, ref, fc1_w, fc1_b, fc2_w, fc2_b)
        corrected = _diffuser(xm * correct_m, ref, qv_w, k_w, proj_w, proj_b, ln_g, ln_b)
        out = correct_m * corrected + (1.0 - correct_m) * xm
        return jnp.concatenate((out, ref), axis=0)

    def _L0_ffn_ref(x, ln1_g, ln1_b, qkv_w, qkv_b, proj_w, proj_b, ln2_g, ln2_b, gate_w, w1, b1, w2, b2):
        import jax, jax.numpy as jnp
        import numpy as np
        DIM = 192
        HEADS = 12
        EXPERTS = 8
        HID = 768
        TOP_K = 2
        LN_EPS = 1e-05

        def _layer_norm(x, g, b):
            mu = x.mean(-1, keepdims=True)
            var = ((x - mu) ** 2).mean(-1, keepdims=True)
            return (x - mu) * jax.lax.rsqrt(var + LN_EPS) * g + b

        def _attention(x, qkv_w, qkv_b, proj_w, proj_b):
            B, N, C = x.shape
            hd = C // HEADS
            qkv = (x @ qkv_w + qkv_b).reshape(B, N, 3, HEADS, hd).transpose(2, 0, 3, 1, 4)
            q, k, v = (qkv[0], qkv[1], qkv[2])
            attn = jax.nn.softmax(jnp.einsum('bhnd,bhmd->bhnm', q, k) * hd ** (-0.5), axis=-1)
            o = jnp.einsum('bhnm,bhmd->bhnd', attn, v).transpose(0, 2, 1, 3).reshape(B, N, C)
            return o @ proj_w + proj_b

        def _moe_mlp(xn, gate_w, w1, b1, w2, b2):
            T = xn.shape[0]
            logits = xn @ gate_w
            top_logits, top_idx = jax.lax.top_k(logits, TOP_K)
            top_gates = jax.nn.softmax(top_logits, axis=-1)
            gates = jnp.zeros((T, EXPERTS), xn.dtype).at[jnp.arange(T)[:, None], top_idx].set(top_gates)
            h = jax.nn.gelu(jnp.einsum('td,edh->teh', xn, w1) + b1, approximate=False)
            y = jnp.einsum('teh,ehd->ted', h, w2) + b2
            return jnp.einsum('ted,te->td', y, gates)
        B, N, C = x.shape
        x = x + _attention(_layer_norm(x, ln1_g, ln1_b), qkv_w, qkv_b, proj_w, proj_b)
        xn = _layer_norm(x, ln2_g, ln2_b).reshape(B * N, C)
        moe_out = _moe_mlp(xn, gate_w, w1, b1, w2, b2).reshape(B, N, C)
        return x + moe_out
    h = _L0_tok_ref(x, L0_tok_W, L0_tok_b)
    h = _layernorm(h + _L0_attn_ref(h, L0_attn_qv_w, L0_attn_k_w, L0_attn_proj_w, L0_attn_proj_b, L0_attn_ln_g, L0_attn_ln_b, L0_attn_fc1_w, L0_attn_fc1_b, L0_attn_fc2_w, L0_attn_fc2_b), axis=-1)
    h = _layernorm(h + _L0_ffn_ref(h, L0_ffn_ln1_g, L0_ffn_ln1_b, L0_ffn_qkv_w, L0_ffn_qkv_b, L0_ffn_proj_w, L0_ffn_proj_b, L0_ffn_ln2_g, L0_ffn_ln2_b, L0_ffn_gate_w, L0_ffn_w1, L0_ffn_b1, L0_ffn_w2, L0_ffn_b2), axis=-1)
    return h

_drawn_inputs = setup_inputs


def setup_inputs(seed=0):
    import zlib

    import numpy as np

    out = dict(_drawn_inputs(seed))
    spreads = {'L0_tok_b': (0.0, 0.1),
     'L0_attn_proj_b': (0.0, 0.1),
     'L0_attn_ln_g': (1.0, 0.2),
     'L0_attn_ln_b': (0.0, 0.1),
     'L0_attn_fc1_b': (0.0, 0.1),
     'L0_attn_fc2_b': (0.0, 0.1),
     'L0_ffn_ln1_g': (1.0, 0.6),
     'L0_ffn_ln1_b': (0.0, 0.8),
     'L0_ffn_qkv_b': (0.0, 0.456),
     'L0_ffn_proj_b': (0.0, 0.1),
     'L0_ffn_ln2_g': (1.0, 0.6),
     'L0_ffn_ln2_b': (0.0, 0.59),
     'L0_ffn_b1': (0.0, 0.73),
     'L0_ffn_b2': (0.0, 0.271)}
    factors = {'L0_ffn_qkv_w': 4.27, 'L0_ffn_proj_w': 2.823}
    for name, (base, spread) in spreads.items():
        noise = np.random.default_rng([zlib.crc32(name.encode()), seed]).standard_normal(out[name].shape)
        drawn = base * np.exp(spread * noise) if base else spread * noise
        out[name] = jnp.asarray(drawn.astype(out[name].dtype))
    for name, factor in factors.items():
        out[name] = (out[name] * factor).astype(out[name].dtype)
    return out
```

```python
from contextlib import ExitStack

import concourse.bass as bass
from concourse import mybir

ALU = mybir.AluOpType
ACT = mybir.ActivationFunctionType
F32 = mybir.dt.float32
AX_X = mybir.AxisListType.X

B, N, C = 32, 36, 192
NREF = 10
BM = B - NREF
HEADS, HD = 12, 16
JB = 3
T = JB * N
NT = -(-B // JB)
NTOK = NT * T
MT = -(-BM // JB)
KF = 6
HF = C // 2
E1, E2 = C // 4, C // 8
STEPS = 3
EXP, HID = 8, 768
HJ = HID // 128
EPS = 1e-5
COS_EPS = 1e-8
FIRST_REF = BM * N - (MT - 1) * T
LAST = B * N - (NT - 1) * T
CHUNKS = [(0, 4), (4, 4), (8, 3)]

(V_TOKB, V_APB, V_ALG, V_ALB, V_L1G, V_L1B, V_FPB, V_L2G, V_L2B, V_VB) = range(10)


def vit_kernel(nc, d, out):
    with ExitStack() as ctx:
        def sb(name, shape, dt=F32):
            return ctx.enter_context(nc.sbuf_tensor(name, shape, dt))

        def sem(name):
            return ctx.enter_context(nc.semaphore(name))

        bank = [ctx.enter_context(nc.psum_tensor(f"bank{i}", [128, 512], F32)) for i in range(8)]

        xT = sb("xT", [128, NT, KF, T])
        tokw = sb("tokw", [128, KF, C])
        vecs = sb("vecs", [T, 10, C])
        fc1 = sb("fc1", [HF, 2, E1])
        fc1b = sb("fc1b", [E1, 1])
        fc2 = sb("fc2", [E1, E2])
        fc2b = sb("fc2b", [T, E2])
        kw = sb("kw", [HF, 2, C])
        wqv = sb("wqv", [HF, 2, 2 * C])
        wq = sb("wq", [HF, 2, C])
        wqT = sb("wqT", [HF, 2, C])
        wpa = sb("wpa", [HF, 2, C])
        wqkp = sb("wqkp", [HF, 2, 2, 384])
        wv2 = sb("wv2", [HF, 2, C])
        wpf = sb("wpf", [HF, 2, C])
        qkbm = sb("qkbm", [128, 2, 3, T])
        gate = sb("gate", [HF, 2, EXP])
        w1 = sb("w1", [HF, EXP, 2, HID])
        w2 = sb("w2", [128, EXP, HJ, C])
        b1 = sb("b1", [128, EXP, HJ])
        b2 = sb("b2", [EXP, C])
        ident = sb("ident", [T, T])
        sel = sb("sel", [T, 2, T])
        colm = sb("colm", [HF, JB, T])
        rowm = sb("rowm", [T, 4])
        bdm = sb("bdm", [HF, 2, HF])
        iota8 = sb("iota8", [T, 2, EXP])

        h = sb("h", [T, NT, C])
        hT = sb("hT", [HF, 2, NTOK])
        e1T = sb("e1T", [E1, NTOK])
        ex = sb("ex", [T, NT, E2])
        exs = sb("exs", [T, NT, E2])
        nrm = sb("nrm", [T, NT])
        rb = sb("rb", [T, E2])
        cosm = sb("cosm", [T, MT])
        th = sb("th", [T, MT])
        mask = sb("mask", [T, MT])
        omask = sb("omask", [T, MT])
        kref = sb("kref", [T, 4, C])
        gbd = sb("gbd", [HF, 2, HF])
        epsc = sb("epsc", [128, 1])
        xs = sb("xs", [T, NT, C])
        xTs = sb("xTs", [HF, 2, 2, T])
        spare = xT[:].rearrange("p t k n -> p (t k n)")
        qp = spare[0:T, 0:384].rearrange("p (b c) -> p b c", b=2)
        vm = spare[0:T, 384:1536].rearrange("p (b f j c) -> p b f j c", b=2, f=2, j=JB)
        qTm = spare[0:HF, 1536:2832].rearrange("p (b f j c) -> p b f j c", b=2, f=2, j=JB)
        osb = spare[0:T, 2832:3600].rearrange("p (b c) -> p b c", b=4)
        oc = spare[0:T, 3600:4368].rearrange("p (b c) -> p b c", b=4)
        rm = sb("rm", [HF, 2, JB, HF])
        ocT = sb("ocT", [HF, 2, T])
        ln_in = sb("ln_in", [T, C])
        stats = sb("stats", [T, 6])
        mv = sb("mv", [T, 2])
        std = sb("std", [T, 1])
        rstd = sb("rstd", [T, 1])
        lnt = sb("lnt", [T, C])
        h1 = xs
        x1 = sb("x1", [T, 2, C])
        x1T = sb("x1T", [HF, 2, T])
        qkT = sb("qkT", [128, 2, 3, T])
        v2 = sb("v2", [T, C])
        s_max = sb("s_max", [T, HEADS])
        prob = spare[0:T, 0:HEADS * T].rearrange("p (u m) -> p u m", u=HEADS)
        psm = sb("psm", [T, HEADS])
        prec = sb("prec", [T, HEADS])
        probT = spare[0:T, HEADS * T:2 * HEADS * T].rearrange("p (u m) -> p u m", u=HEADS)
        ao = sb("ao", [T, C])
        aoT = sb("aoT", [HF, 2, T])
        base = h
        xn = sb("xn", [T, 2, C])
        xnT = hT
        lg = sb("lg", [T, NT, EXP])
        m1 = sb("m1", [T, NT, EXP])
        m2 = sb("m2", [T, NT, EXP])
        lt = sb("lt", [T, NT, EXP])
        gts = sb("gts", [T, NT, EXP])
        vv = sb("vv", [T, 6, NT])
        gT = spare[0:EXP, 5500:5500 + NT * T].rearrange("p (t n) -> p t n", t=NT)
        hidT = spare[:, 0:2 * HJ * 4 * T].rearrange("p (b j n) -> p b j n", b=2, j=HJ)

        scratch = nc.dram_tensor("scratch", [MT, JB * HEADS * N * HD], F32, kind="Internal").ap()

        x_in = [sem(f"x_in{t}") for t in range(NT)]
        early_in = sem("early_in")
        attn_in = sem("attn_in")
        ffn_in = sem("ffn_in")
        exp_in = [sem(f"exp_in{e}") for e in range(EXP)]
        oc_loaded = [sem(f"oc_loaded{i}") for i in range(4)]
        S = {}
        for name in ("eps_ready tok_psum h_ready hT_psum hT_ready e1_psum e1_ready ex_psum sq_ready nrm_ready "
                     "exn_ready rb_psum cos_ready th_ready mask_ready k_psum k_ready g_psum g_ready wqg_psum wqg_ready "
                     "xs_ready xT_psum xT_ready qT_psum qv_psum qp_ready vm_ready qTm_ready r_psum rm_ready o_psum "
                     "o_ready o_stored ocT_psum ocT_ready y_psum y_read var_ready std_ready "
                     "x1_ready x1T_psum x1T_ready qk_psum qk_ready v_psum v_ready s_psum s_shifted p_exp p_ready "
                     "pT_psum pT_ready ao_psum ao_ready aoT_psum aoT_ready pr_psum xn_ready xnT_psum xnT_ready "
                     "lg_psum gex_in gex_ready gts_ready gT_psum gT_ready b2_psum b2_read hid_psum hid_ready ye_psum ye_read "
                     "out_ready out_stored dve_chain").split():
            S[name] = sem(name)

        block = ctx.enter_context(nc.Block())
        NI = STEPS * MT
        EARLY = ["tokw", "vecs", "fc1", "fc1b", "fc2", "fc2b", "ident", "sel", "rowm", "kw", "wqT", "bdm"]
        DIFF = ["wq", "wqv", "colm", "wpa"]
        FFN = ["wqkp", "wv2", "wpf", "qkbm", "gate", "b1", "b2", "iota8"]
        tiles = dict(tokw=tokw, vecs=vecs, fc1=fc1, fc1b=fc1b, fc2=fc2, fc2b=fc2b, ident=ident, sel=sel, rowm=rowm,
                     kw=kw, wqT=wqT, bdm=bdm, wq=wq, wqv=wqv, colm=colm, wpa=wpa, wqkp=wqkp, wv2=wv2, wpf=wpf,
                     qkbm=qkbm, gate=gate, b1=b1, b2=b2, iota8=iota8)

        @block.sync
        def _(sp):
            sp.dma_start(tokw[:], d["tokw"]).then_inc(early_in, 16)
            for t in range(2):
                sp.dma_start(xT[:, t], d["xT"][t]).then_inc(x_in[t], 16)
            for name in EARLY[1:]:
                sp.dma_start(tiles[name][:], d[name]).then_inc(early_in, 16)
            for t in range(2, NT):
                sp.dma_start(xT[:, t], d["xT"][t]).then_inc(x_in[t], 16)
            for name in DIFF:
                sp.dma_start(tiles[name][:], d[name]).then_inc(attn_in, 16)
            for name in FFN:
                sp.dma_start(tiles[name][:], d[name]).then_inc(ffn_in, 16)
            for e in range(EXP):
                sp.dma_start(w1[:, e], d["w1"][e]).then_inc(exp_in[e], 16)
                sp.dma_start(w2[:, e], d["w2"][e]).then_inc(exp_in[e], 16)
            for i in range(NI):
                t = i % MT
                sp.wait_ge(S["o_ready"], i + 1)
                for j in range(JB):
                    sp.dma_start(scratch[t].rearrange("(j h n d) -> j n h d", j=JB, h=HEADS, n=N)[j],
                                 osb[j * N:(j + 1) * N, i % 4].rearrange("p (h d) -> p h d", h=HEADS)
                                 ).then_inc(S["o_stored"], 16)
                sp.wait_ge(S["o_stored"], 16 * JB * (i + 1))
                if i >= 4:
                    sp.wait_ge(S["ocT_psum"], i - 3)
                sp.dma_start(oc[:, i % 4], scratch[t].rearrange("(p c) -> p c", p=T)).then_inc(oc_loaded[i % 4], 16)
            out_tiles = out.rearrange("b n c -> (b n) c")
            for t in range(NT):
                rows = T if t < NT - 1 else LAST
                sp.wait_ge(S["out_ready"], t + 1)
                sp.dma_start(out_tiles[t * T:t * T + rows], h1[0:rows, t]).then_inc(S["out_stored"], 16)
            sp.wait_ge(S["out_stored"], 16 * NT)

        @block.tensor
        def _(pe):
            def mm(o, l, r, start=True, stop=True):
                return nc.tensor.matmul(o, l, r, start=start, stop=stop)

            def turn(o, i):
                for f in range(2):
                    last = nc.tensor.transpose(o[:, f, :], i[:, f * HF:(f + 1) * HF], ident[:])
                return last

            def halves(b):
                return bank[b][0:HF, 0:2 * T].rearrange("p (f t) -> p f t", f=2)

            pe.wait_ge(early_in, 16 * len(EARLY))
            for t in range(NT + 1):
                if t < NT:
                    pe.wait_ge(x_in[t], 16)
                    if t >= 2:
                        pe.wait_ge(S["h_ready"], t - 1)
                    for k in range(KF):
                        last = mm(bank[t % 2][0:T, 0:C], xT[:, t, k, :], tokw[:, k, :], k == 0, k == KF - 1)
                    last.then_inc(S["tok_psum"], 1)
                if t >= 1:
                    pe.wait_ge(S["h_ready"], t)
                    if t >= 3:
                        pe.wait_ge(S["hT_ready"], t - 2)
                    turn(halves(2 + (t - 1) % 2), h[:, t - 1]).then_inc(S["hT_psum"], 1)
            for c, (t0, n) in enumerate(CHUNKS):
                pe.wait_ge(S["hT_ready"], t0 + n)
                for k in range(2):
                    last = mm(bank[4 + c][0:E1, 0:n * T], fc1[:, k, :], hT[:, k, t0 * T:(t0 + n) * T], k == 0, k == 1)
                last.then_inc(S["e1_psum"], 1)
            for i in range(4):
                t = MT - 1 + i
                for k in range(2):
                    last = mm(bank[i][0:T, 0:C], hT[:, k, t * T:(t + 1) * T], kw[:, k, :], k == 0, k == 1)
                last.then_inc(S["k_psum"], 1)
            pe.wait_ge(S["e1_ready"], len(CHUNKS))
            for t in range(NT):
                last = mm(bank[7][0:T, t * E2:(t + 1) * E2], e1T[:, t * T:(t + 1) * T], fc2[:])
            last.then_inc(S["ex_psum"], 1)
            pe.wait_ge(S["k_ready"], 4)
            for f in range(2):
                for i in range(4):
                    rows = T if i < 3 else LAST
                    a = kref[0:rows, i, f * HF:(f + 1) * HF]
                    last = mm(bank[2][0:HF, f * HF:(f + 1) * HF], a, a, i == 0, i == 3)
            last.then_inc(S["g_psum"], 1)
            pe.wait_ge(S["g_ready"], 1)
            for k in range(2):
                for f in range(2):
                    last = mm(bank[3][0:HF, k * C + f * HF:k * C + (f + 1) * HF],
                              wqT[:, f, k * HF:(k + 1) * HF], gbd[:, f, :])
            last.then_inc(S["wqg_psum"], 1)
            pe.wait_ge(S["exn_ready"], 1)
            for i in range(4):
                rows = T if i < 3 else LAST
                last = mm(bank[6][0:T, 0:E2], sel[0:rows, int(i > 0), :], ex[0:rows, MT - 1 + i, :], i == 0, i == 3)
            last.then_inc(S["rb_psum"], 1)

            pe.wait_ge(attn_in, 16 * len(DIFF))
            pe.wait_ge(S["wqg_ready"], 1)
            for i in range(NI + 5):
                if i < NI:
                    pe.wait_ge(S["xs_ready"], i + 1)
                    if i >= 1:
                        pe.wait_ge(S["xT_ready"], i)
                    turn(halves(0), xs[:, i % MT]).then_inc(S["xT_psum"], 1)
                if 1 <= i <= NI:
                    q = i - 1
                    pe.wait_ge(S["qp_ready"], q + 1)
                    pe.wait_ge(S["vm_ready"], q + 1)
                    if q >= 1:
                        pe.wait_ge(S["rm_ready"], q)
                    for f in range(2):
                        last = mm(bank[3 + f][0:HF, 0:JB * HF], qp[:, q % 2, f * HF:(f + 1) * HF], vm[:, q % 2, f].rearrange("p j c -> p (j c)"))
                    last.then_inc(S["r_psum"], 1)
                if i < NI:
                    pe.wait_ge(S["xT_ready"], i + 1)
                    if i >= 1:
                        pe.wait_ge(S["qTm_ready"], i)
                        pe.wait_ge(S["vm_ready"], i)
                    for f in range(2):
                        for k in range(2):
                            last = mm(bank[1][0:HF, f * T:(f + 1) * T], wq[:, k, f * HF:(f + 1) * HF], xTs[:, i % 2, k, :], k == 0, k == 1)
                    last.then_inc(S["qT_psum"], 1)
                    for k in range(2):
                        last = mm(bank[2][0:T, 0:2 * C], xTs[:, i % 2, k, :], wqv[:, k, :], k == 0, k == 1)
                    last.then_inc(S["qv_psum"], 1)
                if 1 <= i <= NI:
                    q = i - 1
                    pe.wait_ge(S["rm_ready"], q + 1)
                    pe.wait_ge(S["qTm_ready"], q + 1)
                    if q >= 1:
                        pe.wait_ge(S["o_ready"], q)
                    for f in range(2):
                        for j in range(JB):
                            last = mm(bank[5][0:T, f * HF:(f + 1) * HF], qTm[:, q % 2, f, j, :], rm[:, f, j, :], j == 0, j == JB - 1)
                    last.then_inc(S["o_psum"], 1)
                if i >= 5:
                    q = i - 5
                    pe.wait_ge(oc_loaded[q % 4], 16 * (q // 4 + 1))
                    turn(halves(6), oc[:, q % 4]).then_inc(S["ocT_psum"], 1)
                    pe.wait_ge(S["ocT_ready"], q + 1)
                    if q >= 1:
                        pe.wait_ge(S["y_read"], q)
                    for k in range(2):
                        last = mm(bank[7][0:T, 0:C], ocT[:, k, :], wpa[:, k, :], k == 0, k == 1)
                    last.then_inc(S["y_psum"], 1)

            pe.wait_ge(ffn_in, 16 * len(FFN))

            def after_attention(t):
                pe.wait_ge(S["ao_ready"], t + 1)
                turn(halves(0), ao[:]).then_inc(S["aoT_psum"], 1)
                pe.wait_ge(S["aoT_ready"], t + 1)
                for k in range(2):
                    last = mm(bank[7][0:T, 0:C], aoT[:, k, :], wpf[:, k, :], k == 0, k == 1)
                last.then_inc(S["pr_psum"], 1)
                pe.wait_ge(S["xn_ready"], t + 1)
                turn(halves(0), xn[:, t % 2]).then_inc(S["xnT_psum"], 1)
                pe.wait_ge(S["xnT_ready"], t + 1)

            for t in range(NT):
                pe.wait_ge(S["x1_ready"], t + 1)
                turn(halves(0), x1[:, t % 2]).then_inc(S["x1T_psum"], 1)
                pe.wait_ge(S["x1T_ready"], t + 1)
                for a in range(2):
                    for g in range(3):
                        for k in range(2):
                            last = mm(bank[5 + a][:, g * T:(g + 1) * T], wqkp[:, k, a, g * 128:(g + 1) * 128], x1T[:, k, :], k == 0, k == 1)
                last.then_inc(S["qk_psum"], 1)
                for k in range(2):
                    last = mm(bank[7][0:T, 0:C], x1T[:, k, :], wv2[:, k, :], k == 0, k == 1)
                last.then_inc(S["v_psum"], 1)
                pe.wait_ge(S["qk_ready"], t + 1)
                for g in range(3):
                    for r in range(4):
                        rows = slice(32 * r, 32 * r + 32)
                        last = mm(bank[1 + r][0:T, g * T:(g + 1) * T], qkT[rows, 0, g, :], qkT[rows, 1, g, :])
                last.then_inc(S["s_psum"], 1)
                pe.wait_ge(S["p_exp"], t + 1)
                for r in range(4):
                    for g in range(3):
                        last = nc.tensor.transpose(bank[1 + r][0:T, g * T:(g + 1) * T], prob[:, 3 * r + g, :], ident[:])
                    last.then_inc(S["pT_psum"], 1)
                pe.wait_ge(S["pT_ready"], 4 * (t + 1))
                pe.wait_ge(S["v_ready"], t + 1)
                for hh in range(HEADS):
                    last = mm(bank[0][0:T, hh * HD:(hh + 1) * HD], probT[:, hh, :], v2[:, hh * HD:(hh + 1) * HD])
                last.then_inc(S["ao_psum"], 1)
                after_attention(t)
            for t in range(NT):
                for k in range(2):
                    last = mm(bank[0][0:T, t * EXP:(t + 1) * EXP], xnT[:, k, t * T:(t + 1) * T], gate[:, k, :], k == 0, k == 1)
            last.then_inc(S["lg_psum"], 1)
            pe.wait_ge(S["gts_ready"], 1)
            for t in range(NT):
                last = nc.tensor.transpose(bank[1 + t // 4][0:EXP, (t % 4) * T:(t % 4 + 1) * T], gts[:, t, :], ident[:])
            last.then_inc(S["gT_psum"], 1)
            pe.wait_ge(S["gT_ready"], 1)
            for t in range(NT):
                if t >= 2:
                    pe.wait_ge(S["b2_read"], t - 1)
                mm(bank[6 + t % 2][0:T, 0:C], gT[:, t, :], b2[:]).then_inc(S["b2_psum"], 1)

            def second(i):
                e, (t0, n) = i // 3, CHUNKS[i % 3]
                pe.wait_ge(S["hid_ready"], HJ * (i + 1))
                for u in range(n):
                    y = e * NT + t0 + u
                    if y < 2:
                        pe.wait_ge(S["b2_read"], NT)
                    else:
                        pe.wait_ge(S["ye_read"], y - 1)
                    for j in range(HJ):
                        last = mm(bank[6 + y % 2][0:T, 0:C], hidT[:, i % 2, j, u * T:(u + 1) * T], w2[:, e, j, :], j == 0, j == HJ - 1)
                    last.then_inc(S["ye_psum"], 1)

            for i in range(3 * EXP + 1):
                if i < 3 * EXP:
                    e, (t0, n) = i // 3, CHUNKS[i % 3]
                    if i % 3 == 0:
                        pe.wait_ge(exp_in[e], 32)
                    for j in range(HJ):
                        m = i * HJ + j
                        if m >= 4:
                            pe.wait_ge(S["hid_ready"], m - 3)
                        for k in range(2):
                            last = mm(bank[2 + m % 4][:, 0:n * T], w1[:, e, k, j * 128:(j + 1) * 128], xnT[:, k, t0 * T:(t0 + n) * T], k == 0, k == 1)
                        last.then_inc(S["hid_psum"], 1)
                if i >= 1:
                    second(i - 1)

        @block.scalar
        def _(act):
            def copy(o, i):
                return nc.scalar.activation(o, i, ACT.Copy)

            def halves(b):
                return bank[b][0:HF, 0:2 * T].rearrange("p (f t) -> p f t", f=2)

            act.wait_ge(S["eps_ready"], 1)
            for t in range(NT):
                act.wait_ge(S["hT_psum"], t + 1)
                copy(hT[:, :, t * T:(t + 1) * T], halves(2 + t % 2)).then_inc(S["hT_ready"], 1)
            for c, (t0, n) in enumerate(CHUNKS):
                act.wait_ge(S["e1_psum"], c + 1)
                nc.scalar.activation(e1T[:, t0 * T:(t0 + n) * T], bank[4 + c][0:E1, 0:n * T], ACT.Gelu, bias=fc1b[:, 0:1]).then_inc(S["e1_ready"], 1)
            for i in range(4):
                act.wait_ge(S["k_psum"], i + 1)
                src = bank[i][0:T, 0:C]
                if i == 0:
                    nc.scalar.activation(kref[:, i, :], src, ACT.Copy, scale=rowm[:, 3:4]).then_inc(S["k_ready"], 1)
                else:
                    copy(kref[:, i, :], src).then_inc(S["k_ready"], 1)
            act.wait_ge(S["sq_ready"], 1)
            nc.scalar.activation(nrm[:], nrm[:], ACT.Sqrt).then_inc(S["nrm_ready"], 1)
            act.wait_ge(S["cos_ready"], 1)
            nc.scalar.activation(th[:], cosm[:], ACT.Tanh, scale=12.5).then_inc(S["th_ready"], 1)

            def sqrt_var(n):
                act.wait_ge(S["var_ready"], n)
                nc.scalar.activation(std[:], mv[:, 1:2], ACT.Sqrt, bias=epsc[0:T, 0:1]).then_inc(S["std_ready"], 1)

            for i in range(NI + 5):
                if i < NI:
                    act.wait_ge(S["xT_psum"], i + 1)
                    if i >= 2:
                        act.wait_ge(S["qv_psum"], i - 1)
                    copy(xTs[:, i % 2], halves(0)).then_inc(S["xT_ready"], 1)
                    act.wait_ge(S["qv_psum"], i + 1)
                    if i >= 2:
                        act.wait_ge(S["r_psum"], i - 1)
                    copy(qp[:, i % 2], bank[2][0:T, 0:C]).then_inc(S["qp_ready"], 1)
                    for j in range(JB):
                        last = nc.scalar.activation(vm[:, i % 2, :, j, :], bank[2][0:T, C:2 * C].rearrange("p (f c) -> p f c", f=2), ACT.Copy, scale=rowm[:, j:j + 1])
                    last.then_inc(S["vm_ready"], 1)
                if 1 <= i <= NI:
                    q = i - 1
                    act.wait_ge(S["o_psum"], q + 1)
                    if q >= 4:
                        act.wait_ge(S["o_stored"], 16 * JB * (q - 3))
                    copy(osb[:, q % 4], bank[5][0:T, 0:C]).then_inc(S["o_ready"], 1)
                if i >= 5:
                    q = i - 5
                    act.wait_ge(S["ocT_psum"], q + 1)
                    if q >= 1:
                        act.wait_ge(S["y_psum"], q)
                    copy(ocT[:], halves(6)).then_inc(S["ocT_ready"], 1)
                    sqrt_var(q + 1)

            n_ln = NI
            for t in range(NT):
                sqrt_var(n_ln + 1)
                sqrt_var(n_ln + 2)
                n_ln += 2
                act.wait_ge(S["x1T_psum"], t + 1)
                copy(x1T[:], halves(0)).then_inc(S["x1T_ready"], 1)
                act.wait_ge(S["v_psum"], t + 1)
                copy(v2[:], bank[7][0:T, 0:C]).then_inc(S["v_ready"], 1)
                act.wait_ge(S["s_shifted"], t + 1)
                nc.scalar.activation(prob, prob, ACT.Exp, scale=float(HD) ** -0.5).then_inc(S["p_exp"], 1)
                for r in (1, 3):
                    act.wait_ge(S["pT_psum"], 4 * t + r + 1)
                    copy(probT[:, 3 * r:3 * r + 3, :].rearrange("p a b -> p (a b)"), bank[1 + r][0:T, 0:3 * T]).then_inc(S["pT_ready"], 1)
                act.wait_ge(S["aoT_psum"], t + 1)
                copy(aoT[:], halves(0)).then_inc(S["aoT_ready"], 1)
                sqrt_var(n_ln + 1)
                n_ln += 1
                act.wait_ge(S["xnT_psum"], t + 1)
                copy(xnT[:, :, t * T:(t + 1) * T], halves(0)).then_inc(S["xnT_ready"], 1)
            act.wait_ge(S["gex_in"], 1)
            nc.scalar.activation(vv[:, 3, :], vv[:, 2, :], ACT.Exp).then_inc(S["gex_ready"], 1)
            act.wait_ge(S["gT_psum"], 1)
            for c, (t0, n) in enumerate(CHUNKS):
                last = copy(gT[:, t0:t0 + n, :].rearrange("p a b -> p (a b)"), bank[1 + c][0:EXP, 0:n * T])
            last.then_inc(S["gT_ready"], 1)
            for i in range(3 * EXP):
                e, (t0, n) = i // 3, CHUNKS[i % 3]
                if i >= 2:
                    act.wait_ge(S["ye_psum"], ((i - 2) // 3) * NT + CHUNKS[(i - 2) % 3][0] + CHUNKS[(i - 2) % 3][1])
                for j in range(HJ):
                    m = i * HJ + j
                    act.wait_ge(S["hid_psum"], m + 1)
                    nc.scalar.activation(hidT[:, i % 2, j, 0:n * T], bank[2 + m % 4][:, 0:n * T], ACT.Gelu, bias=b1[:, e, j:j + 1]).then_inc(S["hid_ready"], 1)
            for t in range(NT):
                sqrt_var(n_ln + 1)
                n_ln += 1

        @block.vector
        def _(dve):
            V = nc.vector
            chain = [0]
            n_ln = [0]

            def link(ins):
                chain[0] += 1
                ins.then_inc(S["dve_chain"], 1)
                dve.wait_ge(S["dve_chain"], chain[0])

            def vec(v):
                return vecs[:, v, :]

            def layernorm(o, x, gain=None, shift=None):
                link(V.bn_stats(stats[:], x))
                n_ln[0] += 1
                V.bn_aggr(mv[:], stats[:]).then_inc(S["var_ready"], 1)
                dve.wait_ge(S["var_ready"], n_ln[0])
                dve.wait_ge(S["std_ready"], n_ln[0])
                link(V.reciprocal(rstd[:], std[:]))
                if gain is None:
                    return V.tensor_scalar(o, x, mv[:, 0:1], rstd[:, 0:1], ALU.subtract, ALU.mult)
                link(V.tensor_scalar(lnt[:], x, mv[:, 0:1], rstd[:, 0:1], ALU.subtract, ALU.mult))
                link(V.tensor_tensor(lnt[:], lnt[:], vec(gain), ALU.mult))
                return V.tensor_tensor(o, lnt[:], vec(shift), ALU.add)

            V.memset(epsc[:], EPS).then_inc(S["eps_ready"], 1)
            dve.wait_ge(early_in, 16 * len(EARLY))
            for t in range(NT):
                dve.wait_ge(S["tok_psum"], t + 1)
                V.tensor_tensor(h[:, t], bank[t % 2][0:T, 0:C], vec(V_TOKB), ALU.add).then_inc(S["h_ready"], 1)
            dve.wait_ge(S["ex_psum"], 1)
            link(V.tensor_tensor(ex[:], bank[7][0:T, 0:NT * E2].rearrange("p (t e) -> p t e", t=NT),
                                 fc2b[:, None, :].broadcast_to([T, NT, E2]), ALU.add))
            link(V.tensor_tensor(exs[:], ex[:], ex[:], ALU.mult))
            V.tensor_reduce(nrm[:], exs[:], AX_X, ALU.add).then_inc(S["sq_ready"], 1)
            dve.wait_ge(S["g_psum"], 1)
            V.tensor_tensor(gbd[:], bank[2][0:HF, 0:C].rearrange("p (f c) -> p f c", f=2),
                            bdm[:, 1:2, :].broadcast_to([HF, 2, HF]), ALU.mult).then_inc(S["g_ready"], 1)
            dve.wait_ge(S["wqg_psum"], 1)
            dve.wait_ge(attn_in, 16 * len(DIFF))
            V.tensor_copy(wqv[:, :, 0:C], bank[3][0:HF, 0:2 * C].rearrange("p (k c) -> p k c", k=2)).then_inc(S["wqg_ready"], 1)
            dve.wait_ge(S["nrm_ready"], 1)
            link(V.tensor_scalar(nrm[:], nrm[:], COS_EPS, None, ALU.max))
            link(V.reciprocal(nrm[:], nrm[:]))
            V.tensor_tensor(ex[:], ex[:], nrm[:, :, None].broadcast_to([T, NT, E2]), ALU.mult).then_inc(S["exn_ready"], 1)
            dve.wait_ge(S["rb_psum"], 1)
            dve.wait_ge(S["exn_ready"], 1)
            link(V.tensor_copy(rb[:], bank[6][0:T, 0:E2]))
            link(V.tensor_tensor(exs[:, 0:MT], ex[:, 0:MT], rb[:, None, :].broadcast_to([T, MT, E2]), ALU.mult))
            V.tensor_reduce(cosm[:], exs[:, 0:MT], AX_X, ALU.add).then_inc(S["cos_ready"], 1)
            dve.wait_ge(S["th_ready"], 1)
            link(V.tensor_scalar(mask[:], th[:], 0.5, 0.5, ALU.mult, ALU.add))
            link(V.tensor_scalar(omask[:], mask[:], -1.0, 1.0, ALU.mult, ALU.add))
            for t in range(MT):
                V.tensor_scalar(xs[:, t], h[:, t], mask[:, t:t + 1], None, ALU.mult).then_inc(S["xs_ready"], 1)

            for i in range(NI + 5):
                if i < NI:
                    dve.wait_ge(S["qT_psum"], i + 1)
                    if i >= 2:
                        dve.wait_ge(S["o_psum"], i - 1)
                    for f in range(2):
                        last = V.tensor_tensor(qTm[:, i % 2, f], bank[1][0:HF, f * T:(f + 1) * T][:, None, :].broadcast_to([HF, JB, T]), colm[:], ALU.mult)
                    last.then_inc(S["qTm_ready"], 1)
                if 1 <= i <= NI:
                    q = i - 1
                    dve.wait_ge(S["r_psum"], q + 1)
                    if q >= 1:
                        dve.wait_ge(S["o_psum"], q)
                    for f in range(2):
                        last = V.tensor_tensor(rm[:, f], bank[3 + f][0:HF, 0:JB * HF].rearrange("p (j c) -> p j c", j=JB),
                                               bdm[:, 0:1, :].broadcast_to([HF, JB, HF]), ALU.mult)
                    last.then_inc(S["rm_ready"], 1)
                if i >= 5:
                    q = i - 5
                    dve.wait_ge(S["y_psum"], q + 1)
                    V.tensor_tensor(ln_in[:], bank[7][0:T, 0:C], vec(V_APB), ALU.add).then_inc(S["y_read"], 1)
                    dve.wait_ge(S["y_read"], q + 1)
                    if q < NI - MT:
                        dve.wait_ge(S["xT_psum"], q + 1)
                    layernorm(xs[:, q % MT], ln_in[:], V_ALG, V_ALB).then_inc(S["xs_ready"], 1)
            dve.wait_ge(S["xs_ready"], MT + NI)
            dve.wait_ge(ffn_in, 16 * len(FFN))
            for t in range(NT):
                if t < MT:
                    link(V.tensor_scalar(ln_in[:], xs[:, t], mask[:, t:t + 1], None, ALU.mult))
                    link(V.scalar_tensor_tensor(out=ln_in[:], in0=h[:, t], scalar=omask[:, t:t + 1], in1=ln_in[:], op0=ALU.mult, op1=ALU.add))
                    link(V.tensor_tensor(ln_in[:], ln_in[:], h[:, t], ALU.add))
                if t >= MT:
                    link(V.tensor_scalar(ln_in[:], h[:, t], 2.0, None, ALU.mult))
                if t == MT - 1:
                    link(V.tensor_tensor(lnt[:], h[:, t], h[:, t], ALU.add))
                    link(V.tensor_scalar(lnt[:], lnt[:], rowm[:, 3:4], None, ALU.mult))
                    link(V.scalar_tensor_tensor(out=ln_in[:], in0=ln_in[:], scalar=rowm[:, 0:1], in1=lnt[:], op0=ALU.mult, op1=ALU.add))
                link(layernorm(h1[:, t], ln_in[:]))
                if t >= 2:
                    dve.wait_ge(S["x1T_psum"], t - 1)
                layernorm(x1[:, t % 2], h1[:, t], V_L1G, V_L1B).then_inc(S["x1_ready"], 1)
                dve.wait_ge(S["x1_ready"], t + 1)
                dve.wait_ge(S["qk_psum"], t + 1)
                for a in range(2):
                    last = V.tensor_tensor(qkT[:, a].rearrange("p g t -> p (g t)"), bank[5 + a][:, 0:3 * T], qkbm[:, a].rearrange("p g t -> p (g t)"), ALU.add)
                last.then_inc(S["qk_ready"], 1)
                dve.wait_ge(S["s_psum"], t + 1)
                for r in range(4):
                    last = V.tensor_reduce(s_max[:, 3 * r:3 * r + 3], bank[1 + r][0:T, 0:3 * T].rearrange("p (u m) -> p u m", u=3), AX_X, ALU.max)
                link(last)
                for r in range(4):
                    last = V.tensor_tensor(prob[:, 3 * r:3 * r + 3, :], bank[1 + r][0:T, 0:3 * T].rearrange("p (u m) -> p u m", u=3),
                                           s_max[:, 3 * r:3 * r + 3, None].broadcast_to([T, 3, T]), ALU.subtract)
                last.then_inc(S["s_shifted"], 1)
                dve.wait_ge(S["p_exp"], t + 1)
                link(V.tensor_reduce(psm[:], prob, AX_X, ALU.add))
                link(V.reciprocal(prec[:], psm[:]))
                for r in (0, 2):
                    dve.wait_ge(S["pT_psum"], 4 * t + r + 1)
                    V.tensor_copy(probT[:, 3 * r:3 * r + 3, :].rearrange("p a b -> p (a b)"), bank[1 + r][0:T, 0:3 * T]).then_inc(S["pT_ready"], 1)
                dve.wait_ge(S["ao_psum"], t + 1)
                link(V.tensor_tensor(ao[:].rearrange("p (u m) -> p u m", u=HEADS), bank[0][0:T, 0:C].rearrange("p (u m) -> p u m", u=HEADS),
                                     prec[:, :, None].broadcast_to([T, HEADS, HD]), ALU.mult))
                V.tensor_tensor(ao[:], ao[:], vec(V_VB), ALU.add).then_inc(S["ao_ready"], 1)
                dve.wait_ge(S["pr_psum"], t + 1)
                link(V.tensor_tensor(ln_in[:], bank[7][0:T, 0:C], vec(V_FPB), ALU.add))
                link(V.tensor_tensor(ln_in[:], ln_in[:], h1[:, t], ALU.add))
                V.tensor_tensor(base[:, t], ln_in[:], h1[:, t], ALU.add)
                if t >= 2:
                    dve.wait_ge(S["xnT_psum"], t - 1)
                layernorm(xn[:, t % 2], ln_in[:], V_L2G, V_L2B).then_inc(S["xn_ready"], 1)
                dve.wait_ge(S["xn_ready"], t + 1)

            dve.wait_ge(S["lg_psum"], 1)
            link(V.tensor_copy(lg[:], bank[0][0:T, 0:NT * EXP].rearrange("p (t e) -> p t e", t=NT)))

            def wide(v):
                return v[:, :, None].broadcast_to([T, NT, EXP])

            def rows8(k):
                return iota8[:, k:k + 1, :].broadcast_to([T, NT, EXP])

            for n, m in ((0, m1), (1, m2)):
                link(V.tensor_reduce(vv[:, n, :], lg[:], AX_X, ALU.max))
                link(V.tensor_tensor(m[:], lg[:], wide(vv[:, n, :]), ALU.is_equal))
                link(V.tensor_tensor(lt[:], m[:], rows8(1), ALU.mult))
                link(V.tensor_reduce(vv[:, 4, :], lt[:], AX_X, ALU.min))
                link(V.tensor_tensor(m[:], rows8(1), wide(vv[:, 4, :]), ALU.is_equal))
                if n == 0:
                    link(V.tensor_scalar(lt[:], m[:], -3.0e38, None, ALU.mult))
                    link(V.scalar_tensor_tensor(out=lg[:], in0=lt[:], scalar=0.0, in1=lg[:], op0=ALU.add, op1=ALU.add))
            V.tensor_tensor(vv[:, 2, :], vv[:, 1, :], vv[:, 0, :], ALU.subtract).then_inc(S["gex_in"], 1)
            dve.wait_ge(S["gex_ready"], 1)
            link(V.tensor_scalar(vv[:, 4, :], vv[:, 3, :], 1.0, None, ALU.add))
            link(V.reciprocal(vv[:, 4, :], vv[:, 4, :]))
            link(V.tensor_tensor(vv[:, 5, :], vv[:, 3, :], vv[:, 4, :], ALU.mult))
            link(V.tensor_tensor(m1[:], m1[:], wide(vv[:, 4, :]), ALU.mult))
            link(V.tensor_tensor(m2[:], m2[:], wide(vv[:, 5, :]), ALU.mult))
            V.tensor_tensor(gts[:], m1[:], m2[:], ALU.add).then_inc(S["gts_ready"], 1)
            dve.wait_ge(S["gts_ready"], 1)
            for t in range(NT):
                dve.wait_ge(S["b2_psum"], t + 1)
                V.tensor_tensor(base[:, t], bank[6 + t % 2][0:T, 0:C], base[:, t], ALU.add).then_inc(S["b2_read"], 1)
            dve.wait_ge(S["b2_read"], NT)
            for y in range(EXP * NT):
                e, t = y // NT, y % NT
                dve.wait_ge(S["ye_psum"], y + 1)
                if e:
                    dve.wait_ge(S["ye_read"], y - NT + 1)
                V.scalar_tensor_tensor(out=base[:, t], in0=bank[6 + y % 2][0:T, 0:C], scalar=gts[:, t, e:e + 1], in1=base[:, t],
                                       op0=ALU.mult, op1=ALU.add).then_inc(S["ye_read"], 1)
            dve.wait_ge(S["ye_read"], EXP * NT)
            for t in range(NT):
                layernorm(h1[:, t], base[:, t]).then_inc(S["out_ready"], 1)
                dve.wait_ge(S["out_ready"], t + 1)


def kernel(**inputs):
    import numpy as np
    import concourse.bacc as bacc
    from concourse.bass_utils import run_bass_kernel_spmd

    a = {k.replace("L0_", ""): np.asarray(v) for k, v in inputs.items()}

    def halves(w):
        return w.reshape(2, HF, -1).transpose(1, 0, 2)

    x = np.zeros((NT * JB, N, KF * 128), np.float32)
    x[:B] = a["x"].reshape(B, 3, 6, 16, 6, 16).transpose(0, 2, 4, 1, 3, 5).reshape(B, N, -1)
    image = np.arange(T) // N
    place = np.arange(T) % N
    head = np.arange(HF) // HD
    same = (place[:, None] == place[None, :]) * np.float32(1.0 / NREF)
    sel = np.stack([same * (np.arange(T) >= FIRST_REF)[:, None], same], 1)
    qkv_w, qkv_b = a["ffn_qkv_w"], a["ffn_qkv_b"]
    wqkp = np.zeros((C, 2, HEADS, 32), np.float32)
    order = np.arange(HEADS).reshape(4, 3).T.reshape(-1)
    wqkp[:, :, :, :HD] = qkv_w[:, :2 * C].reshape(C, 2, HEADS, HD)[:, :, order]
    qkbm = np.zeros((2, 3, 4, 32, T), np.float32)
    qkbm[:, :, :, :HD] = qkv_b[:2 * C].reshape(2, HEADS, HD)[:, order].reshape(2, 3, 4, HD)[..., None]
    for j in range(JB):
        qkbm[0, :, :, HD + j] = image != j
        qkbm[1, :, :, HD + j] = np.where(image == j, np.float32(-2.0 ** 100), np.float32(0))
    vec = [a["tok_b"], a["attn_proj_b"], a["attn_ln_g"], a["attn_ln_b"], a["ffn_ln1_g"], a["ffn_ln1_b"],
           a["ffn_proj_b"], a["ffn_ln2_g"], a["ffn_ln2_b"], qkv_b[2 * C:]]
    e = np.arange(EXP)
    data = {
        "xT": x.reshape(NT, T, KF, 128).transpose(0, 3, 2, 1),
        "tokw": a["tok_W"].reshape(C, KF, 128).transpose(2, 1, 0),
        "vecs": np.broadcast_to(np.stack(vec)[None], (T, 10, C)),
        "fc1": halves(a["attn_fc1_w"]), "fc1b": a["attn_fc1_b"][:, None], "fc2": a["attn_fc2_w"],
        "fc2b": np.broadcast_to(a["attn_fc2_b"][None], (T, E2)),
        "kw": halves(a["attn_k_w"]), "wqv": halves(a["attn_qv_w"]),
        "wq": halves(a["attn_qv_w"][:, :C]), "wqT": halves(a["attn_qv_w"][:, :C].T),
        "wpa": halves(a["attn_proj_w"]),
        "wqkp": halves(wqkp.reshape(C, -1)).reshape(HF, 2, 2, 384), "wv2": halves(qkv_w[:, 2 * C:]),
        "wpf": halves(a["ffn_proj_w"]),
        "qkbm": qkbm.reshape(2, 3, 128, T).transpose(2, 0, 1, 3),
        "gate": halves(a["ffn_gate_w"]),
        "w1": a["ffn_w1"].reshape(EXP, 2, HF, HID).transpose(0, 2, 1, 3),
        "w2": a["ffn_w2"].reshape(EXP, HJ, 128, C).transpose(0, 2, 1, 3),
        "b1": a["ffn_b1"].reshape(EXP, HJ, 128).transpose(2, 0, 1), "b2": a["ffn_b2"],
        "ident": np.eye(T), "sel": sel,
        "colm": np.broadcast_to((image[None] == np.arange(JB)[:, None])[None], (HF, JB, T)),
        "rowm": np.stack([image == 0, image == 1, image == 2, np.arange(T) >= FIRST_REF], 1),
        "bdm": np.stack([(head[:, None] == head[None]) * 1.0, (head[:, None] == head[None]) / (HD * NREF)], 1),
        "iota8": np.broadcast_to(np.stack([e, e - EXP])[None], (T, 2, EXP)),
    }
    nc = bacc.Bacc("TRN2", target_bir_lowering=False, num_devices=1)
    arrays, aps = {}, {}
    for name, v in data.items():
        v = np.ascontiguousarray(v, dtype=np.float32)
        arrays["in_" + name] = v
        aps[name] = nc.dram_tensor("in_" + name, v.shape, F32, kind="ExternalInput").ap()
    out = nc.dram_tensor("out", (B, N, C), F32, kind="ExternalOutput").ap()
    vit_kernel(nc, aps, out)
    r = run_bass_kernel_spmd(nc, [arrays], core_ids=[0])
    return r.results[0]["out"]
```

```python
from contextlib import ExitStack

import concourse.bass as bass
from concourse import mybir

ALU = mybir.AluOpType
ACT = mybir.ActivationFunctionType
F32 = mybir.dt.float32
F16 = mybir.dt.float16
BF16 = mybir.dt.bfloat16
AX_X = mybir.AxisListType.X

B, N, C = 32, 36, 192
NREF = 10
BM = B - NREF
HEADS, HD = 12, 16
JB = 3
T = JB * N
NT = -(-B // JB)
NTOK = NT * T
MT = -(-BM // JB)
KF = 6
HF = C // 2
E1, E2 = C // 4, C // 8
STEPS = 3
EXP, HID = 8, 768
HJ = HID // 128
EPS = 1e-5
SCALE = float(HD) ** -0.5
COS_EPS = 1e-8
FIRST_REF = BM * N - (MT - 1) * T
LAST = B * N - (NT - 1) * T
CHUNKS = [(0, 4), (4, 4), (8, 3)]
P = 128
ET = B * N // P
EC = 3
NC = ET // EC
PASSES = ((0, 0), (0, 1), (1, 0))
PIECES = 3 * EXP

V_TOKB, V_APB, V_ALG, V_ALB, V_FPB = range(5)
G_DIFF, G_LN1, G_LN2 = range(3)


def vit_kernel(nc, d, out):
    with ExitStack() as ctx:
        def sb(name, shape, dt=F32):
            return ctx.enter_context(nc.sbuf_tensor(name, shape, dt))

        def sem(name):
            return ctx.enter_context(nc.semaphore(name))

        bank = [ctx.enter_context(nc.psum_tensor(f"bank{i}", [128, 512], F32)) for i in range(8)]

        xT = sb("xT", [128, NT, KF, T])
        tokw = sb("tokw", [128, KF, C])
        vecs = sb("vecs", [T, 5, C])
        gains = sb("gains", [HF, 3, 2, 2])
        vbb = sb("vbb", [HF, 2, T])
        fc1 = sb("fc1", [HF, 2, E1])
        fc1b = sb("fc1b", [E1, 1])
        fc2 = sb("fc2", [E1, E2])
        fc2b = sb("fc2b", [T, E2])
        kw = sb("kw", [HF, 2, C])
        wqv = sb("wqv", [HF, 2, 2 * C])
        wq = sb("wq", [HF, 2, C])
        wqT = sb("wqT", [HF, 2, C])
        wpa = sb("wpa", [HF, 2, C])
        wqkp = sb("wqkp", [HF, 2, 2, 384])
        wv2 = sb("wv2", [HF, 2, C])
        wpf = sb("wpf", [HF, 2, C])
        qkbm = sb("qkbm", [128, 2, 3, T])
        gate = sb("gate", [HF, 2, EXP])
        w1h, w1l = sb("w1h", [HF, EXP, 2, HID], F16), sb("w1l", [HF, EXP, 2, HID], BF16)
        w2h, w2l = sb("w2h", [P, EXP, HJ, C], F16), sb("w2l", [P, EXP, HJ, C], BF16)
        b1 = sb("b1", [128, EXP, HJ])
        b2 = sb("b2", [EXP, C])
        ident = sb("ident", [P, P])
        sel = sb("sel", [T, 2, T])
        colm = sb("colm", [HF, JB, T])
        rowm = sb("rowm", [T, 4])
        bdm = sb("bdm", [HF, 2, HF])
        iota8 = sb("iota8", [P, 2, EXP])

        h_all = sb("h", [P, NT, C])
        h = h_all[0:T]
        hT = sb("hT", [HF, 2, NTOK])
        e1T = sb("e1T", [E1, NTOK])
        ex = sb("ex", [T, NT, E2])
        exs = sb("exs", [T, NT, E2])
        nrm = sb("nrm", [T, NT])
        rb = sb("rb", [T, E2])
        cosm = sb("cosm", [T, MT])
        th = sb("th", [T, MT])
        mask = sb("mask", [T, MT])
        mask2 = sb("mask2", [T, MT])
        gbd = sb("gbd", [HF, 2, HF])
        xs_all = sb("xs", [P, NT, C])
        xs = xs_all[0:T]
        xTs = sb("xTs", [HF, 2, 2, T])
        spare = xT[:].rearrange("p t k n -> p (t k n)")
        qp = spare[0:T, 0:384].rearrange("p (b c) -> p b c", b=2)
        vm = spare[0:T, 384:1536].rearrange("p (b f j c) -> p b f j c", b=2, f=2, j=JB)
        qTm = spare[0:HF, 1536:2832].rearrange("p (b f j c) -> p b f j c", b=2, f=2, j=JB)
        osb = spare[0:T, 2832:3600].rearrange("p (b c) -> p b c", b=4)
        oc = spare[0:T, 3600:4368].rearrange("p (b c) -> p b c", b=4)
        kref = spare[0:T, 2832:3600].rearrange("p (b c) -> p b c", b=4)
        stage = spare[:, 4400:4400 + 2 * HJ * C].rearrange("p (b c) -> p b c", b=2)
        rm = sb("rm", [HF, 2, JB, HF])
        ocT = sb("ocT", [HF, 2, T])
        yb = sb("yb", [T, 2, C])
        stats = sb("stats", [P, 6])
        mv = sb("mv", [P, 4, 2])
        veps = sb("veps", [P, 1])
        nhalf = sb("nhalf", [P, 1])
        rstd = sb("rstd", [P, 4])
        rstd1 = sb("rstd1", [T, 4])
        fbias = sb("fbias", [T, C])
        h1 = xs
        hb = sb("hb", [T, 2, C])
        x1 = sb("x1", [T, 2, C])
        x1T = sb("x1T", [HF, 2, 2, T])
        qkT = spare[:, 2592:3240].rearrange("p (a g t) -> p a g t", a=2, g=3)
        v2 = spare[0:T, 3240:3648].rearrange("p (b u d) -> p b u d", b=2, u=HEADS)
        s_max = sb("s_max", [T, HEADS])
        prob = spare[0:T, 0:HEADS * T].rearrange("p (u m) -> p u m", u=HEADS)
        nmax = sb("nmax", [T, HEADS])
        prec = sb("prec", [T, HEADS])
        probT = spare[0:T, HEADS * T:2 * HEADS * T].rearrange("p (u m) -> p u m", u=HEADS)
        ao = spare[0:T, 3648:4032].rearrange("p (b c) -> p b c", b=2)
        aoT = sb("aoT", [HF, 2, T])
        base = sb("base", [T, 2, C])
        xn = sb("xn", [T, 2, C])
        xnT = hT
        xnh, xnl = sb("xnh", [HF, 2, NTOK], F16), sb("xnl", [HF, 2, NTOK], BF16)
        acc = h_all[:, 0:ET]
        res = xs_all[:, 0:ET]
        lg = sb("lg", [P, ET, EXP])
        m1 = sb("m1", [P, ET, EXP])
        m2 = sb("m2", [P, ET, EXP])
        lt = sb("lt", [P, ET, EXP])
        gts = sb("gts", [P, ET, EXP])
        vv = sb("vv", [P, 6, ET])
        gT = e1T[0:EXP, 0:ET * P].rearrange("p (t n) -> p t n", t=ET)
        NH = 4
        hidf = spare[:, 0:NH * EC * P].rearrange("p (b n) -> p b n", b=NH)
        parts = spare[:, NH * EC * P:NH * EC * P + 2 * HJ * EC * P]
        hidh = parts[:, 0:HJ * EC * P].bitcast(F16).rearrange("p (b j n) -> p b j n", b=2, j=HJ)
        hidl = parts[:, HJ * EC * P:2 * HJ * EC * P].bitcast(BF16).rearrange("p (b j n) -> p b j n", b=2, j=HJ)

        res_dram = nc.dram_tensor("res_dram", [NTOK, C], F32, kind="Internal").ap()
        SCR = MT
        scratch = nc.dram_tensor("scratch", [SCR, JB * HEADS * N * HD], F32, kind="Internal").ap()

        x_in = [sem(f"x_in{t}") for t in range(NT)]
        tokw_in = sem("tokw_in")
        early_in = sem("early_in")
        attn_in = sem("attn_in")
        ffn_in = sem("ffn_in")
        piece_in = [sem(f"piece_in{b}") for b in range(2)]
        base_stored = [sem(f"base_stored{b}") for b in range(2)]
        o_stored = [sem(f"o_stored{i}") for i in range(2)]
        oc_loaded = [sem(f"oc_loaded{i}") for i in range(4)]
        S = {}
        for name in ("tok_psum h_ready hT_psum hT_ready e1_psum e1_ready ex_psum sq_ready nrm_ready "
                     "exn_ready rb_psum cos_ready th_ready k_psum k_ready g_psum g_ready wqg_psum wqg_ready "
                     "xs_ready xT_psum xT_ready qT_psum qv_psum qp_ready vm_ready qTm_ready r_psum rm_ready o_psum "
                     "o_ready ocT_psum ocT_ready y_psum y_read var_ready std_ready pool_chain "
                     "fb_psum fb_ready ones_ready x1_ready h1_ready x1T_psum x1T_ready qk_psum qk_ready v_psum v_ready "
                     "s_psum nmax_ready p_exp pT_psum pT_dve pT_act ao_psum ao_ready aoT_psum aoT_ready pr_psum "
                     "res_ready hb_ready base_ready xn_ready xnT_psum xnT_ready "
                     "lg_psum gex_in gex_ready gts_ready gT_psum gT_ready b2_psum b2_read hid_psum hid_ready ye_psum "
                     "ye_read high_ready low_ready hidh_ready hidl_ready xnh_ready xnl_ready acc_ready res_loaded out_ready out_stored dve_chain").split():
            S[name] = sem(name)

        block = ctx.enter_context(nc.Block())
        NI = STEPS * MT

        def weights(q, low):
            e, k = q // 3, q % 3
            if k < 2:
                return (w1h, w1l)[low][:, e, k, :], stage[0:HF, q % 2, 0:HID]
            return (w2h, w2l)[low][:, e].rearrange("p j c -> p (j c)"), stage[:, q % 2, :]

        EARLY = ["vecs", "fc1", "fc1b", "fc2", "fc2b", "ident", "sel", "rowm", "kw", "wqT", "bdm"]
        DIFF = ["wq", "wqv", "colm", "wpa", "gains"]
        FFN = ["wqkp", "wv2", "wpf", "vbb", "qkbm", "gate", "b1", "b2", "iota8"]
        tiles = dict(gains=gains, vbb=vbb, vecs=vecs, fc1=fc1, fc1b=fc1b, fc2=fc2, fc2b=fc2b, ident=ident, sel=sel, rowm=rowm,
                     kw=kw, wqT=wqT, bdm=bdm, wq=wq, wqv=wqv, colm=colm, wpa=wpa, wqkp=wqkp, wv2=wv2, wpf=wpf,
                     qkbm=qkbm, gate=gate, b1=b1, b2=b2, iota8=iota8)

        @block.sync
        def _(sp):
            sp.dma_start(tokw[:], d["tokw"]).then_inc(tokw_in, 16)
            for t in range(2):
                sp.dma_start(xT[:, t], d["xT"][t]).then_inc(x_in[t], 16)
            for name in EARLY:
                sp.dma_start(tiles[name][:], d[name]).then_inc(early_in, 16)
            for t in range(2, NT):
                sp.dma_start(xT[:, t], d["xT"][t]).then_inc(x_in[t], 16)
            for name in DIFF:
                sp.dma_start(tiles[name][:], d[name]).then_inc(attn_in, 16)
            for name in FFN:
                sp.dma_start(tiles[name][:], d[name]).then_inc(ffn_in, 16)
            sp.wait_ge(S["tok_psum"], NT)
            for i in range(NI + 1):
                if i < NI:
                    sp.wait_ge(S["o_ready"], i + 1)
                    for j in range(JB):
                        sp.dma_start(scratch[i % SCR].rearrange("(j h n d) -> j n h d", j=JB, h=HEADS, n=N)[j],
                                     osb[j * N:(j + 1) * N, i % 4].rearrange("p (h d) -> p h d", h=HEADS)
                                     ).then_inc(o_stored[i % 2], 16)
                if i >= 1:
                    q = i - 1
                    sp.wait_ge(o_stored[q % 2], 16 * JB * (q // 2 + 1))
                    if q >= 4:
                        sp.wait_ge(S["ocT_psum"], q - 3)
                    sp.dma_start(oc[:, q % 4], scratch[q % SCR].rearrange("(p c) -> p c", p=T)).then_inc(oc_loaded[q % 4], 16)
                if i < PIECES:
                    e, k = i // 3, i % 3
                    if i >= 2:
                        sp.wait_ge(S["low_ready"], i - 1)
                    if k < 2:
                        sp.dma_start(stage[0:HF, i % 2, 0:HID], d["w1"][e, :, k]).then_inc(piece_in[i % 2], 16)
                    else:
                        sp.dma_start(stage[:, i % 2, :], d["w2"][e]).then_inc(piece_in[i % 2], 16)
            for t in range(NT):
                sp.wait_ge(S["base_ready"], t + 1)
                sp.dma_start(res_dram[t * T:(t + 1) * T], base[:, t % 2]).then_inc(base_stored[t % 2], 16)
            sp.wait_ge(base_stored[0], 16 * ((NT + 1) // 2))
            sp.wait_ge(base_stored[1], 16 * (NT // 2))
            sp.dma_start(res, res_dram[0:ET * P].rearrange("(t p) c -> p t c", p=P)).then_inc(S["res_loaded"], 16)
            out_tiles = out.rearrange("b n c -> (b n) c")
            for t in range(ET):
                sp.wait_ge(S["out_ready"], t + 1)
                sp.dma_start(out_tiles[t * P:(t + 1) * P], res[:, t]).then_inc(S["out_stored"], 16)
            sp.wait_ge(S["out_stored"], 16 * ET)

        @block.tensor
        def _(pe):
            def mm(o, l, r, start=True, stop=True):
                return nc.tensor.matmul(o, l, r, start=start, stop=stop)

            def turn(o, i):
                for f in range(2):
                    last = nc.tensor.transpose(o[:, f, :], i[:, f * HF:(f + 1) * HF], ident[0:T, 0:T])
                return last

            def halves(b):
                return bank[b][0:HF, 0:2 * T].rearrange("p (f t) -> p f t", f=2)

            halves2 = bank[0][0:HF, 2 * T:4 * T].rearrange("p (f t) -> p f t", f=2)

            pe.wait_ge(tokw_in, 16)
            for t in range(NT + 1):
                if t == 1:
                    pe.wait_ge(early_in, 16 * len(EARLY))
                if t < NT:
                    pe.wait_ge(x_in[t], 16)
                    if t >= 2:
                        pe.wait_ge(S["h_ready"], t - 1)
                    for k in range(KF):
                        last = mm(bank[t % 2][0:T, 0:C], xT[:, t, k, :], tokw[:, k, :], k == 0, k == KF - 1)
                    last.then_inc(S["tok_psum"], 1)
                if t >= 1:
                    pe.wait_ge(S["h_ready"], t)
                    if t >= 3:
                        pe.wait_ge(S["hT_ready"], t - 2)
                    turn(halves(2 + (t - 1) % 2), h[:, t - 1]).then_inc(S["hT_psum"], 1)
            for c, (t0, n) in enumerate(CHUNKS):
                pe.wait_ge(S["hT_ready"], t0 + n)
                for k in range(2):
                    last = mm(bank[4 + c][0:E1, 0:n * T], fc1[:, k, :], hT[:, k, t0 * T:(t0 + n) * T], k == 0, k == 1)
                last.then_inc(S["e1_psum"], 1)
            for i in range(4):
                t = MT - 1 + i
                for k in range(2):
                    last = mm(bank[i][0:T, 0:C], hT[:, k, t * T:(t + 1) * T], kw[:, k, :], k == 0, k == 1)
                last.then_inc(S["k_psum"], 1)
            pe.wait_ge(S["e1_ready"], len(CHUNKS))
            for t in range(NT):
                last = mm(bank[7][0:T, t * E2:(t + 1) * E2], e1T[:, t * T:(t + 1) * T], fc2[:])
            last.then_inc(S["ex_psum"], 1)
            pe.wait_ge(S["k_ready"], 4)
            for f in range(2):
                for i in range(4):
                    rows = T if i < 3 else LAST
                    a = kref[0:rows, i, f * HF:(f + 1) * HF]
                    last = mm(bank[2][0:HF, f * HF:(f + 1) * HF], a, a, i == 0, i == 3)
            last.then_inc(S["g_psum"], 1)
            pe.wait_ge(S["g_ready"], 1)
            for k in range(2):
                for f in range(2):
                    last = mm(bank[3][0:HF, k * C + f * HF:k * C + (f + 1) * HF],
                              wqT[:, f, k * HF:(k + 1) * HF], gbd[:, f, :])
            last.then_inc(S["wqg_psum"], 1)
            pe.wait_ge(S["exn_ready"], 1)
            for i in range(4):
                rows = T if i < 3 else LAST
                last = mm(bank[6][0:T, 0:E2], sel[0:rows, int(i > 0), :], ex[0:rows, MT - 1 + i, :], i == 0, i == 3)
            last.then_inc(S["rb_psum"], 1)

            pe.wait_ge(attn_in, 16 * len(DIFF))
            pe.wait_ge(S["wqg_ready"], 1)
            for i in range(NI + 5):
                q = i - 1
                if i < NI:
                    pe.wait_ge(S["xs_ready"], i + 1)
                    turn(halves(0), xs[:, i % MT]).then_inc(S["xT_psum"], 1)
                if 1 <= i <= NI:
                    pe.wait_ge(S["qp_ready"], q + 1)
                    pe.wait_ge(S["vm_ready"], q + 1)
                    if q >= 1:
                        pe.wait_ge(S["rm_ready"], q)
                    for f in range(2):
                        last = mm(bank[3 + f][0:HF, 0:JB * HF], qp[:, q % 2, f * HF:(f + 1) * HF], vm[:, q % 2, f].rearrange("p j c -> p (j c)"))
                    last.then_inc(S["r_psum"], 1)
                if i < NI:
                    pe.wait_ge(S["xT_ready"], i + 1)
                    if i >= 1:
                        pe.wait_ge(S["qTm_ready"], i)
                    for f in range(2):
                        for k in range(2):
                            last = mm(bank[1][0:HF, f * T:(f + 1) * T], wq[:, k, f * HF:(f + 1) * HF], xTs[:, i % 2, k, :], k == 0, k == 1)
                    last.then_inc(S["qT_psum"], 1)
                    for k in range(2):
                        last = mm(bank[2][0:T, 0:2 * C], xTs[:, i % 2, k, :], wqv[:, k, :], k == 0, k == 1)
                    last.then_inc(S["qv_psum"], 1)
                if i >= 5:
                    p = i - 5
                    pe.wait_ge(oc_loaded[p % 4], 16 * (p // 4 + 1))
                    turn(halves(6), oc[:, p % 4]).then_inc(S["ocT_psum"], 1)
                if 1 <= i <= NI:
                    pe.wait_ge(S["rm_ready"], q + 1)
                    pe.wait_ge(S["qTm_ready"], q + 1)
                    if q >= 1:
                        pe.wait_ge(S["o_ready"], q)
                    for f in range(2):
                        for j in range(JB):
                            last = mm(bank[5][0:T, f * HF:(f + 1) * HF], qTm[:, q % 2, f, j, :], rm[:, f, j, :], j == 0, j == JB - 1)
                    last.then_inc(S["o_psum"], 1)
                if i >= 5:
                    pe.wait_ge(S["ocT_ready"], p + 1)
                    if p >= 1:
                        pe.wait_ge(S["y_read"], p)
                    for k in range(2):
                        last = mm(bank[7][0:T, 0:C], ocT[:, k, :], wpa[:, k, :], k == 0, k == 1)
                    last.then_inc(S["y_psum"], 1)

            def to_columns(t):
                pe.wait_ge(S["x1_ready"], t + 1)
                turn(halves(0), x1[:, t % 2]).then_inc(S["x1T_psum"], 1)

            pe.wait_ge(ffn_in, 16 * len(FFN))
            pe.wait_ge(S["y_read"], NI)
            for k in range(2):
                last = mm(bank[7][0:T, 0:C], vbb[:, k, :], wpf[:, k, :], k == 0, k == 1)
            last.then_inc(S["fb_psum"], 1)
            to_columns(0)
            for i in range(NT + 4):
                if 0 <= i - 3 < NT:
                    t = i - 3
                    pe.wait_ge(S["aoT_ready"], t + 1)
                    pe.wait_ge(S["ao_ready"], min(t + 2, NT))
                    pe.wait_ge(S["fb_ready"], 1)
                    if t >= 1:
                        pe.wait_ge(S["res_ready"], t)
                    for k in range(2):
                        last = mm(bank[7][0:T, 0:C], aoT[:, k, :], wpf[:, k, :], k == 0, k == 1)
                    last.then_inc(S["pr_psum"], 1)
                if i >= 5:
                    pe.wait_ge(S["xnT_ready"], i - 4)
                if i < NT:
                    t = i
                    pe.wait_ge(S["x1T_ready"], t + 1)
                    if t >= 2:
                        pe.wait_ge(S["pT_dve"], 2 * (t - 1))
                        pe.wait_ge(S["pT_act"], 2 * (t - 1))
                    for a in range(2):
                        for g in range(3):
                            for k in range(2):
                                last = mm(bank[5 + a][:, g * T:(g + 1) * T], wqkp[:, k, a, g * 128:(g + 1) * 128], x1T[:, t % 2, k, :], k == 0, k == 1)
                        last.then_inc(S["qk_psum"], 1)
                    for k in range(2):
                        last = mm(bank[0][0:T, 0:C], x1T[:, t % 2, k, :], wv2[:, k, :], k == 0, k == 1)
                    last.then_inc(S["v_psum"], 1)
                if 1 <= i <= NT:
                    t = i - 1
                    pe.wait_ge(S["p_exp"], 4 * (t + 1))
                    pe.wait_ge(S["qk_ready"], 2 * min(i + 1, NT))
                    for r in range(4):
                        if r == 2:
                            pe.wait_ge(S["pT_dve"], 2 * t + 1)
                        if r == 3:
                            pe.wait_ge(S["pT_act"], 2 * t + 1)
                        for g in range(3):
                            last = nc.tensor.transpose(bank[5 + r % 2][0:T, g * T:(g + 1) * T], prob[:, 3 * r + g, :], ident[0:T, 0:T])
                        last.then_inc(S["pT_psum"], 1)
                if i < NT:
                    pe.wait_ge(S["v_ready"], i + 1)
                if i + 1 < NT:
                    to_columns(i + 1)
                if 0 <= i - 2 < NT:
                    t = i - 2
                    pe.wait_ge(S["ao_ready"], t + 1)
                    turn(halves2, ao[:, t % 2]).then_inc(S["aoT_psum"], 1)
                if i < NT:
                    pe.wait_ge(S["qk_ready"], 2 * (i + 1))
                    if i >= 1:
                        pe.wait_ge(S["p_exp"], 4 * i)
                    for g in range(3):
                        for r in range(4):
                            rows = slice(32 * r, 32 * r + 32)
                            last = mm(bank[1 + r][0:T, g * T:(g + 1) * T], qkT[rows, 0, g, :], qkT[rows, 1, g, :])
                    last.then_inc(S["s_psum"], 1)
                if 0 <= i - 4 < NT:
                    t = i - 4
                    pe.wait_ge(S["xn_ready"], t + 1)
                    pe.wait_ge(S["x1T_ready"], min(i + 2, NT))
                    pe.wait_ge(S["aoT_ready"], min(i - 1, NT))
                    turn(halves(0), xn[:, t % 2]).then_inc(S["xnT_psum"], 1)
                if 1 <= i <= NT:
                    t = i - 1
                    pe.wait_ge(S["pT_dve"], 2 * (t + 1))
                    pe.wait_ge(S["pT_act"], 2 * (t + 1))
                    if t >= 2:
                        pe.wait_ge(S["res_ready"], t - 1)
                    for hh in range(HEADS):
                        last = mm(bank[7][0:T, hh * (HD + 1):(hh + 1) * (HD + 1)], probT[:, hh, :], v2[:, t % 2, hh, :])
                    last.then_inc(S["ao_psum"], 1)
            pe.wait_ge(S["xnT_ready"], NT)
            for t in range(ET):
                for k in range(2):
                    last = mm(bank[0][:, t * EXP:(t + 1) * EXP], xnT[:, k, t * P:(t + 1) * P], gate[:, k, :], k == 0, k == 1)
            last.then_inc(S["lg_psum"], 1)

            def first(i):
                e, c = i // NC, i % NC
                cols = slice(c * EC * P, (c + 1) * EC * P)
                for j in range(HJ):
                    m = i * HJ + j
                    if m >= 4:
                        pe.wait_ge(S["hid_ready"], m - 3)
                    for n, (k, (a, b)) in enumerate((k, ab) for k in range(2) for ab in PASSES):
                        last = mm(bank[2 + m % 4][:, 0:EC * P], (w1h, w1l)[a][:, e, k, j * P:(j + 1) * P], (xnh, xnl)[b][:, k, cols],
                                  n == 0, n == 5)
                    last.then_inc(S["hid_psum"], 1)

            def second(i):
                e, c = i // NC, i % NC
                pe.wait_ge(S["hidh_ready"], HJ * (i + 1))
                pe.wait_ge(S["hidl_ready"], HJ * (i + 1))
                for u in range(EC):
                    y = i * EC + u
                    if y < 2:
                        pe.wait_ge(S["acc_ready"], ET)
                    else:
                        pe.wait_ge(S["ye_read"], y - 1)
                    for n, (j, (a, b)) in enumerate((j, ab) for j in range(HJ) for ab in PASSES):
                        last = mm(bank[6 + y % 2][:, 0:C], (hidh, hidl)[a][:, i % 2, j, u * P:(u + 1) * P], (w2h, w2l)[b][:, e, j, :],
                                  n == 0, n == 3 * HJ - 1)
                    last.then_inc(S["ye_psum"], 1)

            pe.wait_ge(S["high_ready"], PIECES)
            pe.wait_ge(S["low_ready"], PIECES)
            pe.wait_ge(S["xnh_ready"], NT)
            pe.wait_ge(S["xnl_ready"], NT)
            first(0)
            pe.wait_ge(S["gts_ready"], 1)
            for t in range(ET):
                if t % 4 == 0 and t:
                    pe.wait_ge(S["gT_ready"], t // 4)
                last = nc.tensor.transpose(bank[0][0:EXP, (t % 4) * P:(t % 4 + 1) * P], gts[:, t, :], ident[:])
                if t % 4 == 3 or t == ET - 1:
                    last.then_inc(S["gT_psum"], 1)
            pe.wait_ge(S["gT_ready"], 3)
            for t in range(ET):
                if t >= 2:
                    pe.wait_ge(S["acc_ready"], t - 1)
                mm(bank[6 + t % 2][:, 0:C], gT[:, t, :], b2[:]).then_inc(S["b2_psum"], 1)
            for i in range(1, NC * EXP + 1):
                if i < NC * EXP:
                    first(i)
                second(i - 1)

        @block.scalar
        def _(act):
            def copy(o, i):
                return nc.scalar.activation(o, i, ACT.Copy)

            def halves(b):
                return bank[b][0:HF, 0:2 * T].rearrange("p (f t) -> p f t", f=2)

            halves2 = bank[0][0:HF, 2 * T:4 * T].rearrange("p (f t) -> p f t", f=2)
            for t in range(NT):
                act.wait_ge(S["hT_psum"], t + 1)
                copy(hT[:, :, t * T:(t + 1) * T], halves(2 + t % 2)).then_inc(S["hT_ready"], 1)
            for c, (t0, n) in enumerate(CHUNKS):
                act.wait_ge(S["e1_psum"], c + 1)
                nc.scalar.activation(e1T[:, t0 * T:(t0 + n) * T], bank[4 + c][0:E1, 0:n * T], ACT.Gelu, bias=fc1b[:, 0:1]).then_inc(S["e1_ready"], 1)
            for i in range(4):
                act.wait_ge(S["k_psum"], i + 1)
                src = bank[i][0:T, 0:C]
                if i == 0:
                    nc.scalar.activation(kref[:, i, :], src, ACT.Copy, scale=rowm[:, 3:4]).then_inc(S["k_ready"], 1)
                else:
                    copy(kref[:, i, :], src).then_inc(S["k_ready"], 1)
            act.wait_ge(S["sq_ready"], 1)
            nc.scalar.activation(nrm[:], nrm[:], ACT.Sqrt).then_inc(S["nrm_ready"], 1)
            act.wait_ge(S["cos_ready"], 1)
            nc.scalar.activation(th[:], cosm[:], ACT.Tanh, scale=12.5).then_inc(S["th_ready"], 1)

            def affine(o, i, which):
                for f in range(2):
                    last = nc.scalar.activation(o[:, f], i[:, f], ACT.Identity, scale=gains[:, which, 0, f:f + 1], bias=gains[:, which, 1, f:f + 1])
                return last

            for i in range(NI + 5):
                if i < NI:
                    act.wait_ge(S["xT_psum"], i + 1)
                    if i >= 2:
                        act.wait_ge(S["qv_psum"], i - 1)
                    if i < MT:
                        last = copy(xTs[:, i % 2], halves(0))
                    else:
                        last = affine(xTs[:, i % 2], halves(0), G_DIFF)
                    last.then_inc(S["xT_ready"], 1)
                    act.wait_ge(S["qv_psum"], i + 1)
                    if i >= 2:
                        act.wait_ge(S["r_psum"], i - 1)
                    copy(qp[:, i % 2], bank[2][0:T, 0:C]).then_inc(S["qp_ready"], 1)
                    for j in range(JB):
                        last = nc.scalar.activation(vm[:, i % 2, :, j, :], bank[2][0:T, C:2 * C].rearrange("p (f c) -> p f c", f=2), ACT.Copy, scale=rowm[:, j:j + 1])
                    last.then_inc(S["vm_ready"], 1)
                if i >= 5:
                    q = i - 5
                    act.wait_ge(S["ocT_psum"], q + 1)
                    if q >= 1:
                        act.wait_ge(S["y_psum"], q)
                    copy(ocT[:], halves(6)).then_inc(S["ocT_ready"], 1)
                if 1 <= i <= NI:
                    q = i - 1
                    act.wait_ge(S["o_psum"], q + 1)
                    if q >= 4:
                        act.wait_ge(oc_loaded[q % 4], 16 * (q // 4))
                    copy(osb[:, q % 4], bank[5][0:T, 0:C]).then_inc(S["o_ready"], 1)
                if 3 <= i < PIECES + 3:
                    q = i - 3
                    act.wait_ge(piece_in[q % 2], 16 * (q // 2 + 1))
                    copy(*weights(q, 0)).then_inc(S["high_ready"], 1)

            act.wait_ge(S["ones_ready"], 1)
            act.wait_ge(S["x1T_psum"], 1)
            affine(x1T[:, 0], halves(0), G_LN1).then_inc(S["x1T_ready"], 1)
            for i in range(NT + 4):
                if i < NT:
                    act.wait_ge(S["v_psum"], i + 1)
                    if i >= 2:
                        act.wait_ge(S["ao_psum"], i - 1)
                    copy(v2[:, i % 2, :, 0:HD], bank[0][0:T, 0:C].rearrange("p (u d) -> p u d", u=HEADS)).then_inc(S["v_ready"], 1)
                if 1 <= i <= NT:
                    t = i - 1
                    if t >= 1:
                        act.wait_ge(S["ao_psum"], t)
                    for r in (1, 3):
                        act.wait_ge(S["pT_psum"], 4 * t + r + 1)
                        copy(probT[:, 3 * r:3 * r + 3, :].rearrange("p a b -> p (a b)"), bank[6][0:T, 0:3 * T]).then_inc(S["pT_act"], 1)
                if 0 <= i - 2 < NT:
                    act.wait_ge(S["aoT_psum"], i - 1)
                if i + 1 < NT:
                    act.wait_ge(S["x1T_psum"], i + 2)
                    affine(x1T[:, (i + 1) % 2], halves(0), G_LN1).then_inc(S["x1T_ready"], 1)
                if 0 <= i - 2 < NT:
                    if i >= 3:
                        act.wait_ge(S["pr_psum"], i - 2)
                    copy(aoT[:], halves2).then_inc(S["aoT_ready"], 1)
                if i < NT:
                    if i >= 1:
                        act.wait_ge(S["pT_psum"], 4 * i)
                    for r in range(4):
                        act.wait_ge(S["nmax_ready"], 4 * i + r + 1)
                        for g in range(3):
                            hh = 3 * r + g
                            last = nc.scalar.activation(prob[:, hh, :], bank[1 + r][0:T, g * T:(g + 1) * T], ACT.Exp,
                                                        scale=SCALE, bias=nmax[:, hh:hh + 1])
                        last.then_inc(S["p_exp"], 1)
                if 0 <= i - 4 < NT:
                    t = i - 4
                    act.wait_ge(S["xnT_psum"], t + 1)
                    affine(xnT[:, :, t * T:(t + 1) * T], halves(0), G_LN2).then_inc(S["xnT_ready"], 1)
            def hidden(i0, i1):
                for i in range(i0, i1):
                    e = i // NC
                    for j in range(HJ):
                        m = i * HJ + j
                        act.wait_ge(S["hid_psum"], m + 1)
                        if m >= NH:
                            act.wait_ge(S["hidl_ready"], m - NH + 1)
                        nc.scalar.activation(hidf[:, m % NH], bank[2 + m % 4][:, 0:EC * P], ACT.Gelu, bias=b1[:, e, j:j + 1]).then_inc(S["hid_ready"], 1)

            act.wait_ge(S["gex_in"], 1)
            nc.scalar.activation(vv[:, 3, :], vv[:, 2, :], ACT.Exp).then_inc(S["gex_ready"], 1)
            hidden(0, 1)
            for c in range(3):
                act.wait_ge(S["gT_psum"], c + 1)
                n = min(4, ET - 4 * c)
                copy(gT[:, 4 * c:4 * c + n, :].rearrange("p a b -> p (a b)"), bank[0][0:EXP, 0:n * P]).then_inc(S["gT_ready"], 1)
            hidden(1, NC * EXP)

        @block.vector
        def _(dve):
            V = nc.vector
            chain = [0]
            n_ln = [0]

            def link(ins):
                chain[0] += 1
                ins.then_inc(S["dve_chain"], 1)
                dve.wait_ge(S["dve_chain"], chain[0])

            def vec(v):
                return vecs[:, v, :]

            def moments(x):
                if n_ln[0]:
                    dve.wait_ge(S["var_ready"], n_ln[0])
                link(V.bn_stats(stats[0:x.shape[0]], x))
                n_ln[0] += 1
                V.bn_aggr(mv[0:x.shape[0], (n_ln[0] - 1) % 4], stats[0:x.shape[0]]).then_inc(S["var_ready"], 1)
                return n_ln[0] - 1

            def centred(o, x, n, r=rstd):
                rows = x.shape[0]
                return V.tensor_scalar(o, x, mv[0:rows, n % 4, 0:1], r[0:rows, n % 4:n % 4 + 1], ALU.subtract, ALU.mult)

            dve.wait_ge(early_in, 16 * len(EARLY))
            for t in range(NT):
                dve.wait_ge(S["tok_psum"], t + 1)
                V.tensor_tensor(h[:, t], bank[t % 2][0:T, 0:C], vec(V_TOKB), ALU.add).then_inc(S["h_ready"], 1)
            dve.wait_ge(S["ex_psum"], 1)
            link(V.tensor_tensor(ex[:], bank[7][0:T, 0:NT * E2].rearrange("p (t e) -> p t e", t=NT),
                                 fc2b[:, None, :].broadcast_to([T, NT, E2]), ALU.add))
            link(V.tensor_tensor(exs[:], ex[:], ex[:], ALU.mult))
            V.tensor_reduce(nrm[:], exs[:], AX_X, ALU.add).then_inc(S["sq_ready"], 1)
            dve.wait_ge(S["g_psum"], 1)
            V.tensor_tensor(gbd[:], bank[2][0:HF, 0:C].rearrange("p (f c) -> p f c", f=2),
                            bdm[:, 1:2, :].broadcast_to([HF, 2, HF]), ALU.mult).then_inc(S["g_ready"], 1)
            dve.wait_ge(S["wqg_psum"], 1)
            dve.wait_ge(attn_in, 16 * len(DIFF))
            V.tensor_copy(wqv[:, :, 0:C], bank[3][0:HF, 0:2 * C].rearrange("p (k c) -> p k c", k=2)).then_inc(S["wqg_ready"], 1)
            dve.wait_ge(S["nrm_ready"], 1)
            link(V.tensor_scalar(nrm[:], nrm[:], COS_EPS, None, ALU.max))
            link(V.reciprocal(nrm[:], nrm[:]))
            V.tensor_tensor(ex[:], ex[:], nrm[:, :, None].broadcast_to([T, NT, E2]), ALU.mult).then_inc(S["exn_ready"], 1)
            dve.wait_ge(S["rb_psum"], 1)
            dve.wait_ge(S["exn_ready"], 1)
            link(V.tensor_copy(rb[:], bank[6][0:T, 0:E2]))
            link(V.tensor_tensor(exs[:, 0:MT], ex[:, 0:MT], rb[:, None, :].broadcast_to([T, MT, E2]), ALU.mult))
            V.tensor_reduce(cosm[:], exs[:, 0:MT], AX_X, ALU.add).then_inc(S["cos_ready"], 1)
            dve.wait_ge(S["th_ready"], 1)
            link(V.tensor_scalar(mask[:], th[:], 0.5, 0.5, ALU.mult, ALU.add))
            link(V.tensor_tensor(mask[:, MT - 1:MT], mask[:, MT - 1:MT], rowm[:, 0:1], ALU.mult))
            link(V.tensor_scalar(mask2[:], mask[:], -1.0, 2.0, ALU.mult, ALU.add))
            for t in range(MT):
                V.tensor_scalar(xs[:, t], h[:, t], mask[:, t:t + 1], None, ALU.mult).then_inc(S["xs_ready"], 1)

            for i in range(NI + 6):
                if i < NI:
                    dve.wait_ge(S["qT_psum"], i + 1)
                    if i >= 2:
                        dve.wait_ge(S["o_psum"], i - 1)
                    for f in range(2):
                        last = V.tensor_tensor(qTm[:, i % 2, f], bank[1][0:HF, f * T:(f + 1) * T][:, None, :].broadcast_to([HF, JB, T]), colm[:], ALU.mult)
                    last.then_inc(S["qTm_ready"], 1)
                if 1 <= i <= NI:
                    q = i - 1
                    dve.wait_ge(S["r_psum"], q + 1)
                    if q >= 1:
                        dve.wait_ge(S["o_psum"], q)
                    for f in range(2):
                        last = V.tensor_tensor(rm[:, f], bank[3 + f][0:HF, 0:JB * HF].rearrange("p (j c) -> p j c", j=JB),
                                               bdm[:, 0:1, :].broadcast_to([HF, JB, HF]), ALU.mult)
                    last.then_inc(S["rm_ready"], 1)
                if 5 <= i < NI + 5:
                    q = i - 5
                    dve.wait_ge(S["y_psum"], q + 1)
                    V.tensor_tensor(yb[:, q % 2], bank[7][0:T, 0:C], vec(V_APB), ALU.add).then_inc(S["y_read"], 1)
                    dve.wait_ge(S["y_read"], q + 1)
                    n = moments(yb[:, q % 2])
                    assert n == q
                if i >= 6:
                    q = i - 6
                    dve.wait_ge(S["std_ready"], q + 1)
                    dve.wait_ge(S["xT_psum"], q + 1)
                    if q < NI - MT:
                        centred(xs[:, q % MT], yb[:, q % 2], q).then_inc(S["xs_ready"], 1)
                    else:
                        link(centred(xs[:, q % MT], yb[:, q % 2], q))
                        link(V.tensor_tensor(xs[:, q % MT], xs[:, q % MT], vec(V_ALG), ALU.mult))
                        link(V.tensor_tensor(xs[:, q % MT], xs[:, q % MT], vec(V_ALB), ALU.add))
            V.memset(v2[:, :, :, HD:HD + 1], 1.0).then_inc(S["ones_ready"], 1)
            dve.wait_ge(S["fb_psum"], 1)
            V.tensor_tensor(fbias[:], bank[7][0:T, 0:C], vec(V_FPB), ALU.add).then_inc(S["fb_ready"], 1)
            dve.wait_ge(ffn_in, 16 * len(FFN))

            first = {}

            def combine(t):
                if t < MT:
                    link(V.tensor_scalar(xs[:, t], xs[:, t], mask[:, t:t + 1], None, ALU.mult))
                    link(V.scalar_tensor_tensor(out=xs[:, t], in0=h[:, t], scalar=mask2[:, t:t + 1], in1=xs[:, t], op0=ALU.mult, op1=ALU.add))
                else:
                    link(V.tensor_scalar(xs[:, t], h[:, t], 2.0, None, ALU.mult))
                first[t] = moments(xs[:, t])

            def normalise(t):
                dve.wait_ge(S["std_ready"], first[t] + 1)
                if t >= 2:
                    dve.wait_ge(S["x1T_psum"], t - 1)
                centred(x1[:, t % 2], xs[:, t], first[t], rstd1).then_inc(S["x1_ready"], 1)
                centred(h1[:, t], xs[:, t], first[t]).then_inc(S["h1_ready"], 1)

            def low(t):
                cols = slice(t * T, (t + 1) * T)
                dve.wait_ge(S["xnT_ready"], t + 1)
                V.tensor_copy(xnh[:, :, cols], xnT[:, :, cols]).then_inc(S["xnh_ready"], 1)
                dve.wait_ge(S["xnh_ready"], t + 1)
                V.tensor_tensor(xnl[:, :, cols], xnT[:, :, cols], xnh[:, :, cols], ALU.subtract).then_inc(S["xnl_ready"], 1)

            combine(0)
            normalise(0)
            combine(1)
            normalise(1)
            combine(2)
            for i in range(NT + 3):
                second = None
                if i >= 3:
                    t = i - 3
                    dve.wait_ge(S["pr_psum"], t + 1)
                    dve.wait_ge(S["hb_ready"], t + 1)
                    V.tensor_tensor(yb[:, t % 2], bank[7][0:T, 0:C], hb[:, t % 2], ALU.add).then_inc(S["res_ready"], 1)
                    dve.wait_ge(S["res_ready"], t + 1)
                    if t >= 2:
                        dve.wait_ge(S["base_ready"], t - 1)
                    second = moments(yb[:, t % 2])
                if i < NT:
                    for a in range(2):
                        dve.wait_ge(S["qk_psum"], 2 * i + a + 1)
                        V.tensor_tensor(qkT[:, a].rearrange("p g t -> p (g t)"), bank[5 + a][:, 0:3 * T],
                                        qkbm[:, a].rearrange("p g t -> p (g t)"), ALU.add).then_inc(S["qk_ready"], 1)
                if 1 <= i <= NT:
                    t = i - 1
                    if t >= 1:
                        dve.wait_ge(S["ao_psum"], t)
                    for r in (0, 2):
                        dve.wait_ge(S["pT_psum"], 4 * t + r + 1)
                        V.tensor_copy(probT[:, 3 * r:3 * r + 3, :].rearrange("p a b -> p (a b)"), bank[5][0:T, 0:3 * T]).then_inc(S["pT_dve"], 1)
                if i + 2 < NT:
                    normalise(i + 2)
                if i >= 3:
                    t = i - 3
                    dve.wait_ge(S["std_ready"], second + 1)
                    if t >= 2:
                        dve.wait_ge(S["xnT_psum"], t - 1)
                    centred(xn[:, t % 2], yb[:, t % 2], second).then_inc(S["xn_ready"], 1)
                if i < NT:
                    dve.wait_ge(S["s_psum"], i + 1)
                    for r in range(4):
                        hs = slice(3 * r, 3 * r + 3)
                        link(V.tensor_reduce(s_max[:, hs], bank[1 + r][0:T, 0:3 * T].rearrange("p (u m) -> p u m", u=3), AX_X, ALU.max))
                        V.tensor_scalar(nmax[:, hs], s_max[:, hs], -SCALE, None, ALU.mult).then_inc(S["nmax_ready"], 1)
                if 1 <= i <= NT:
                    t = i - 1
                    dve.wait_ge(S["ao_psum"], t + 1)
                    if t >= 2:
                        dve.wait_ge(S["aoT_psum"], t - 1)
                    heads = bank[7][0:T, 0:HEADS * (HD + 1)].rearrange("p (u d) -> p u d", u=HEADS)
                    link(V.reciprocal(prec[:], heads[:, :, HD]))
                    V.tensor_tensor(ao[:, t % 2].rearrange("p (u d) -> p u d", u=HEADS), heads[:, :, 0:HD],
                                    prec[:, :, None].broadcast_to([T, HEADS, HD]), ALU.mult).then_inc(S["ao_ready"], 1)
                if i + 3 < NT:
                    combine(i + 3)
                if 0 <= i - 5 < NT:
                    low(i - 5)
            for t in range(NT - 2, NT):
                low(t)

            dve.wait_ge(S["lg_psum"], 1)
            link(V.tensor_copy(lg[:], bank[0][:, 0:ET * EXP].rearrange("p (t e) -> p t e", t=ET)))

            def wide(v):
                return v[:, :, None].broadcast_to([P, ET, EXP])

            def rows8(k):
                return iota8[:, k:k + 1, :].broadcast_to([P, ET, EXP])

            for n, m in ((0, m1), (1, m2)):
                link(V.tensor_reduce(vv[:, n, :], lg[:], AX_X, ALU.max))
                link(V.tensor_tensor(m[:], lg[:], wide(vv[:, n, :]), ALU.is_equal))
                link(V.tensor_tensor(lt[:], m[:], rows8(1), ALU.mult))
                link(V.tensor_reduce(vv[:, 4, :], lt[:], AX_X, ALU.min))
                link(V.tensor_tensor(m[:], rows8(1), wide(vv[:, 4, :]), ALU.is_equal))
                if n == 0:
                    link(V.tensor_scalar(lt[:], m[:], -3.0e38, None, ALU.mult))
                    link(V.scalar_tensor_tensor(out=lg[:], in0=lt[:], scalar=0.0, in1=lg[:], op0=ALU.add, op1=ALU.add))
            V.tensor_tensor(vv[:, 2, :], vv[:, 1, :], vv[:, 0, :], ALU.subtract).then_inc(S["gex_in"], 1)
            dve.wait_ge(S["gex_ready"], 1)
            link(V.tensor_scalar(vv[:, 4, :], vv[:, 3, :], 1.0, None, ALU.add))
            link(V.reciprocal(vv[:, 4, :], vv[:, 4, :]))
            link(V.tensor_tensor(vv[:, 5, :], vv[:, 3, :], vv[:, 4, :], ALU.mult))
            link(V.tensor_tensor(m1[:], m1[:], wide(vv[:, 4, :]), ALU.mult))
            link(V.tensor_tensor(m2[:], m2[:], wide(vv[:, 5, :]), ALU.mult))
            V.tensor_tensor(gts[:], m1[:], m2[:], ALU.add).then_inc(S["gts_ready"], 1)
            dve.wait_ge(S["gts_ready"], 1)
            def split(i):
                for j in range(HJ):
                    m = i * HJ + j
                    dve.wait_ge(S["hid_ready"], m + 1)
                    if i >= 2 and j == 0:
                        dve.wait_ge(S["ye_psum"], EC * (i - 1))
                    V.tensor_copy(hidh[:, i % 2, j], hidf[:, m % NH]).then_inc(S["hidh_ready"], 1)
                    dve.wait_ge(S["hidh_ready"], m + 1)
                    V.tensor_tensor(hidl[:, i % 2, j], hidf[:, m % NH], hidh[:, i % 2, j], ALU.subtract).then_inc(S["hidl_ready"], 1)

            split(0)
            for t in range(ET):
                dve.wait_ge(S["b2_psum"], t + 1)
                V.tensor_copy(acc[:, t], bank[6 + t % 2][:, 0:C]).then_inc(S["acc_ready"], 1)
            dve.wait_ge(S["acc_ready"], ET)
            for i in range(1, NC * EXP + 1):
                if i < NC * EXP:
                    split(i)
                e, c = (i - 1) // NC, (i - 1) % NC
                for u in range(EC):
                    y, t = (i - 1) * EC + u, c * EC + u
                    dve.wait_ge(S["ye_psum"], y + 1)
                    if e:
                        dve.wait_ge(S["ye_read"], y - ET + 1)
                    V.scalar_tensor_tensor(out=acc[:, t], in0=bank[6 + y % 2][:, 0:C], scalar=gts[:, t, e:e + 1], in1=acc[:, t],
                                           op0=ALU.mult, op1=ALU.add).then_inc(S["ye_read"], 1)
            dve.wait_ge(S["res_loaded"], 16)
            last_n = {}
            for t in range(ET + 1):
                if t < ET:
                    dve.wait_ge(S["ye_read"], EC * NC * (EXP - 1) + t + 1)
                    link(V.tensor_tensor(acc[:, t], acc[:, t], res[:, t], ALU.add))
                    last_n[t] = moments(acc[:, t])
                if t >= 1:
                    n = last_n[t - 1]
                    dve.wait_ge(S["std_ready"], n + 1)
                    centred(res[:, t - 1], acc[:, t - 1], n).then_inc(S["out_ready"], 1)

        @block.gpsimd
        def _(pool):
            G = nc.gpsimd
            chain, n_ln = [0], [0]

            def link(ins):
                chain[0] += 1
                ins.then_inc(S["pool_chain"], 1)
                pool.wait_ge(S["pool_chain"], chain[0])

            def root(twice=False, rows=T):
                n = n_ln[0]
                k = slice(n % 4, n % 4 + 1)
                n_ln[0] += 1
                var = mv[0:rows, n % 4, 1:2]
                pool.wait_ge(S["var_ready"], n + 1)
                ve = veps[0:rows]
                link(G.tensor_scalar(ve, var, EPS, None, ALU.add))
                last = G.tensor_tensor(rstd[0:rows, k], ve, nhalf[0:rows], ALU.pow)
                if twice:
                    link(last)
                    link(G.tensor_tensor(ve, var, rstd[0:rows, k], ALU.mult))
                    link(G.tensor_tensor(ve, ve, rstd[0:rows, k], ALU.mult))
                    link(G.tensor_scalar(ve, ve, EPS, None, ALU.add))
                    link(G.tensor_tensor(ve, ve, nhalf[0:rows], ALU.pow))
                    last = G.tensor_tensor(rstd1[:, k], ve, rstd[0:rows, k], ALU.mult)
                last.then_inc(S["std_ready"], 1)
                pool.wait_ge(S["std_ready"], n + 1)

            link(G.memset(nhalf[:], -0.5))
            for i in range(5, NI + 5):
                root()
                if i < PIECES + 3:
                    for q in (range(i - 2) if i == 5 else (i - 3,)):
                        o, w = weights(q, 1)
                        pool.wait_ge(S["high_ready"], q + 1)
                        G.tensor_tensor(o, w, weights(q, 0)[0], ALU.subtract).then_inc(S["low_ready"], 1)
            for t in range(3):
                root(twice=True)
            for i in range(NT + 3):
                if 0 <= i - 3 < NT:
                    root()
                    t = i - 3
                    pool.wait_ge(S["res_ready"], t + 1)
                    if t >= 2:
                        pool.wait_ge(base_stored[t % 2], 16 * (t // 2))
                    G.tensor_tensor(base[:, t % 2], yb[:, t % 2], h1[:, t], ALU.add).then_inc(S["base_ready"], 1)
                if i + 3 < NT:
                    root(twice=True)
                if 0 <= i - 2 < NT:
                    t = i - 2
                    pool.wait_ge(S["h1_ready"], t + 1)
                    pool.wait_ge(S["fb_ready"], 1)
                    if t >= 2:
                        pool.wait_ge(S["res_ready"], t - 1)
                    G.tensor_tensor(hb[:, t % 2], h1[:, t], fbias[:], ALU.add).then_inc(S["hb_ready"], 1)
            for t in range(ET):
                root(rows=P)

def kernel(**inputs):
    import numpy as np
    import concourse.bacc as bacc
    from concourse.bass_utils import run_bass_kernel_spmd

    a = {k.replace("L0_", ""): np.asarray(v) for k, v in inputs.items()}

    def halves(w):
        return w.reshape(2, HF, -1).transpose(1, 0, 2)

    x = np.zeros((NT * JB, N, KF * 128), np.float32)
    x[:B] = a["x"].reshape(B, 3, 6, 16, 6, 16).transpose(0, 2, 4, 1, 3, 5).reshape(B, N, -1)
    image = np.arange(T) // N
    place = np.arange(T) % N
    head = np.arange(HF) // HD
    same = (place[:, None] == place[None, :]) * np.float32(1.0 / NREF)
    sel = np.stack([same * (np.arange(T) >= FIRST_REF)[:, None], same], 1)
    qkv_w, qkv_b = a["ffn_qkv_w"], a["ffn_qkv_b"]
    wqkp = np.zeros((C, 2, HEADS, 32), np.float32)
    order = np.arange(HEADS).reshape(4, 3).T.reshape(-1)
    wqkp[:, :, :, :HD] = qkv_w[:, :2 * C].reshape(C, 2, HEADS, HD)[:, :, order]
    qkbm = np.zeros((2, 3, 4, 32, T), np.float32)
    qkbm[:, :, :, :HD] = qkv_b[:2 * C].reshape(2, HEADS, HD)[:, order].reshape(2, 3, 4, HD)[..., None]
    for j in range(JB):
        qkbm[0, :, :, HD + j] = image != j
        qkbm[1, :, :, HD + j] = np.where(image == j, np.float32(-2.0 ** 100), np.float32(0))
    vec = [a["tok_b"], a["attn_proj_b"], a["attn_ln_g"], a["attn_ln_b"], a["ffn_proj_b"]]
    gains = [[a[ln + "_g"], a[ln + "_b"]] for ln in ("attn_ln", "ffn_ln1", "ffn_ln2")]
    e = np.arange(EXP)
    data = {
        "xT": x.reshape(NT, T, KF, 128).transpose(0, 3, 2, 1),
        "tokw": a["tok_W"].reshape(C, KF, 128).transpose(2, 1, 0),
        "vecs": np.broadcast_to(np.stack(vec)[None], (T, 5, C)),
        "gains": np.stack([np.stack(g) for g in gains]).reshape(3, 2, 2, HF).transpose(3, 0, 1, 2),
        "vbb": np.broadcast_to(halves(qkv_b[2 * C:, None]), (HF, 2, T)),
        "fc1": halves(a["attn_fc1_w"]), "fc1b": a["attn_fc1_b"][:, None], "fc2": a["attn_fc2_w"],
        "fc2b": np.broadcast_to(a["attn_fc2_b"][None], (T, E2)),
        "kw": halves(a["attn_k_w"]), "wqv": halves(a["attn_qv_w"]),
        "wq": halves(a["attn_qv_w"][:, :C]), "wqT": halves(a["attn_qv_w"][:, :C].T),
        "wpa": halves(a["attn_proj_w"]),
        "wqkp": halves(wqkp.reshape(C, -1)).reshape(HF, 2, 2, 384), "wv2": halves(qkv_w[:, 2 * C:]),
        "wpf": halves(a["ffn_proj_w"]),
        "qkbm": qkbm.reshape(2, 3, 128, T).transpose(2, 0, 1, 3),
        "gate": halves(a["ffn_gate_w"]),
        "w1": a["ffn_w1"].reshape(EXP, 2, HF, HID).transpose(0, 2, 1, 3),
        "w2": a["ffn_w2"].reshape(EXP, HJ, 128, C).transpose(0, 2, 1, 3),
        "b1": a["ffn_b1"].reshape(EXP, HJ, 128).transpose(2, 0, 1), "b2": a["ffn_b2"],
        "ident": np.eye(P), "sel": sel,
        "colm": np.broadcast_to((image[None] == np.arange(JB)[:, None])[None], (HF, JB, T)),
        "rowm": np.stack([image == 0, image == 1, image == 2, np.arange(T) >= FIRST_REF], 1),
        "bdm": np.stack([(head[:, None] == head[None]) * 1.0, (head[:, None] == head[None]) / (HD * NREF)], 1),
        "iota8": np.broadcast_to(np.stack([e, e - EXP])[None], (P, 2, EXP)),
    }
    nc = bacc.Bacc("TRN2", target_bir_lowering=False, num_devices=1)
    arrays, aps = {}, {}
    for name, v in data.items():
        v = np.ascontiguousarray(v, dtype=np.float32)
        arrays["in_" + name] = v
        aps[name] = nc.dram_tensor("in_" + name, v.shape, F32, kind="ExternalInput").ap()
    out = nc.dram_tensor("out", (B, N, C), F32, kind="ExternalOutput").ap()
    vit_kernel(nc, aps, out)
    r = run_bass_kernel_spmd(nc, [arrays], core_ids=[0])
    return r.results[0]["out"]
```

```python
from contextlib import ExitStack

import concourse.bass as bass
from concourse import mybir

ALU = mybir.AluOpType
ACT = mybir.ActivationFunctionType
F32 = mybir.dt.float32
F16 = mybir.dt.float16
BF16 = mybir.dt.bfloat16
AX_X = mybir.AxisListType.X

B, N, C = 32, 36, 192
NREF = 10
BM = B - NREF
HEADS, HD = 12, 16
JB = 3
T = JB * N
NT = -(-B // JB)
NTOK = NT * T
MT = -(-BM // JB)
KF = 6
HF = C // 2
E1, E2 = C // 4, C // 8
STEPS = 3
EXP, HID = 8, 768
HJ = HID // 128
EPS = 1e-5
SCALE = float(HD) ** -0.5
COS_EPS = 1e-8
FIRST_REF = BM * N - (MT - 1) * T
LAST = B * N - (NT - 1) * T
CHUNKS = [(0, 4), (4, 4), (8, 3)]
P = 128
ET = B * N // P
EC = 3
NC = ET // EC
PASSES = ((0, 0), (0, 1), (1, 0))
PIECES = 3 + 3 * EXP
BAR = 2.0 ** 15

V_TOKB, V_APB, V_ALG, V_ALB, V_FPB = range(5)
G_DIFF, G_LN1, G_LN2 = range(3)


def vit_kernel(nc, d, out):
    with ExitStack() as ctx:
        def sb(name, shape, dt=F32):
            return ctx.enter_context(nc.sbuf_tensor(name, shape, dt))

        def sem(name):
            return ctx.enter_context(nc.semaphore(name))

        bank = [ctx.enter_context(nc.psum_tensor(f"bank{i}", [128, 512], F32)) for i in range(8)]

        xT = sb("xT", [128, NT, KF, T])
        tokw = sb("tokw", [128, KF, C])
        vecs = sb("vecs", [T, 5, C])
        gains = sb("gains", [HF, 3, 2, 2])
        vbh, vbl = sb("vbh", [HF, 2, T], F16), sb("vbl", [HF, 2, T], BF16)
        vbb = sb("vbb", [HF, 2, T])
        fc1 = sb("fc1", [HF, 2, E1])
        fc1b = sb("fc1b", [E1, 1])
        fc2 = sb("fc2", [E1, E2])
        fc2b = sb("fc2b", [T, E2])
        kw = sb("kw", [HF, 2, C])
        wqv = sb("wqv", [HF, 2, 2 * C])
        wq = sb("wq", [HF, 2, C])
        wqT = sb("wqT", [HF, 2, C])
        wpa = sb("wpa", [HF, 2, C])
        wqk = sb("wqkh", [HF, 2, 2, 384], F16), sb("wqkl", [HF, 2, 2, 384], BF16)
        wvp = sb("wvph", [HF, 2, 2, C], F16), sb("wvpl", [HF, 2, 2, C], BF16)
        qkbm = sb("qkbm", [128, 2, 3, T])
        gate = sb("gate", [HF, 2, EXP])
        w1h, w1l = sb("w1h", [HF, EXP, 2, HID], F16), sb("w1l", [HF, EXP, 2, HID], BF16)
        w2h, w2l = sb("w2h", [P, EXP, HJ, C], F16), sb("w2l", [P, EXP, HJ, C], BF16)
        b1 = sb("b1", [128, EXP, HJ])
        b2 = sb("b2", [EXP, C])
        ident = sb("ident", [P, P])
        sel = sb("sel", [T, 2, T])
        colm = sb("colm", [HF, JB, T])
        rowm = sb("rowm", [T, 4])
        bdm = sb("bdm", [HF, 2, HF])
        iota8 = sb("iota8", [P, 2, EXP])

        h_all = sb("h", [P, NT, C])
        h = h_all[0:T]
        hT_all = sb("hT", [P, 2, NTOK])
        hT = hT_all[0:HF]
        e1T = sb("e1T", [E1, NTOK])
        ex = sb("ex", [T, NT, E2])
        exs = sb("exs", [T, NT, E2])
        nrm = sb("nrm", [T, NT])
        rb = sb("rb", [T, E2])
        cosm = sb("cosm", [T, MT])
        th = sb("th", [T, MT])
        mask = sb("mask", [T, MT])
        mask2 = sb("mask2", [T, MT])
        gbd = sb("gbd", [HF, 2, HF])
        xs_all = sb("xs", [P, NT, C])
        xs = xs_all[0:T]
        xTs = sb("xTs", [HF, 2, 2, T])
        spare = xT[:].rearrange("p t k n -> p (t k n)")
        qp = spare[0:T, 0:384].rearrange("p (b c) -> p b c", b=2)
        vm = spare[0:T, 384:1536].rearrange("p (b f j c) -> p b f j c", b=2, f=2, j=JB)
        qTm = spare[0:HF, 1536:2832].rearrange("p (b f j c) -> p b f j c", b=2, f=2, j=JB)
        osb = spare[0:T, 2832:3600].rearrange("p (b c) -> p b c", b=4)
        oc = spare[0:T, 3600:4368].rearrange("p (b c) -> p b c", b=4)
        kref = spare[0:T, 2832:3600].rearrange("p (b c) -> p b c", b=4)
        stage = [spare[:, 4400:4400 + HJ * C], spare[:, 4400 + HJ * C:4400 + 2 * HJ * C]]
        stage += [hT_all[:].rearrange("p k n -> p (k n)")[:, b * HJ * C:(b + 1) * HJ * C] for b in range(2)]
        rm = sb("rm", [HF, 2, JB, HF])
        ocT = sb("ocT", [HF, 2, T])
        yb = sb("yb", [T, 2, C])
        stats = sb("stats", [P, 2, 6])
        mv = sb("mv", [P, 4, 2])
        veps = sb("veps", [P, 1])
        nhalf = sb("nhalf", [P, 1])
        rstd = sb("rstd", [P, 4])
        rstd1 = sb("rstd1", [T, 4])
        fbias = sb("fbias", [T, C])
        h1 = xs
        hb = sb("hb", [T, 2, C])
        x1 = sb("x1", [T, 2, C])
        def at(place, n, rows, dt=F32):
            v = spare[0:rows, place:place + (n if dt == F32 else n // 2)]
            return v if dt == F32 else v.bitcast(dt)

        x1T = at(4680, 2 * T, HF).rearrange("p (f t) -> p f t", f=2)
        x1Th = at(4896, 4 * T, HF, F16).rearrange("p (b f t) -> p b f t", b=2, f=2)
        x1Tl = at(5112, 4 * T, HF, BF16).rearrange("p (b f t) -> p b f t", b=2, f=2)
        aoTh = at(5328, 2 * T, HF, F16).rearrange("p (f t) -> p f t", f=2)
        aoTl = at(5436, 2 * T, HF, BF16).rearrange("p (f t) -> p f t", f=2)
        qkT = at(2592, 6 * T, 128).rearrange("p (a g t) -> p a g t", a=2, g=3)
        qkh = at(3240, 6 * T, 128, F16).rearrange("p (a g t) -> p a g t", a=2, g=3)
        qkl = at(3564, 6 * T, 128, BF16).rearrange("p (a g t) -> p a g t", a=2, g=3)
        v2h = at(3888, 2 * HEADS * (HD + 1), T, F16).rearrange("p (b u d) -> p b u d", b=2, u=HEADS)
        v2l = at(4092, 2 * HEADS * (HD + 1), T, BF16).rearrange("p (b u d) -> p b u d", b=2, u=HEADS)
        prob = spare[0:T, 0:HEADS * T].rearrange("p (u m) -> p u m", u=HEADS)
        nmax = sb("nmax", [T, HEADS])
        prec = sb("prec", [T, HEADS])
        pTh = at(1296, 2 * HEADS * T, T, F16).rearrange("p (b u m) -> p b u m", b=2, u=HEADS)
        pTl = at(5544, 2 * HEADS * T, T, BF16).rearrange("p (b u m) -> p b u m", b=2, u=HEADS)
        ao = spare[0:T, 4296:4680].rearrange("p (b c) -> p b c", b=2)
        base = sb("base", [T, 2, C])
        xn = sb("xn", [T, 2, C])
        xnT = hT
        xnh, xnl = sb("xnh", [HF, 2, NTOK], F16), sb("xnl", [HF, 2, NTOK], BF16)
        acc = h_all[:, 0:ET]
        res = xs_all[:, 0:ET]
        lg = sb("lg", [P, ET, EXP])
        m1 = sb("m1", [P, ET, EXP])
        m2 = sb("m2", [P, ET, EXP])
        lt = sb("lt", [P, ET, EXP])
        gts = sb("gts", [P, ET, EXP])
        vv = sb("vv", [P, 6, ET])
        gT = e1T[0:EXP, 0:ET * P].rearrange("p (t n) -> p t n", t=ET)
        NH = 4
        hidf = spare[:, 0:NH * EC * P].rearrange("p (b n) -> p b n", b=NH)
        parts = spare[:, NH * EC * P:NH * EC * P + 2 * HJ * EC * P]
        hidh = parts[:, 0:HJ * EC * P].bitcast(F16).rearrange("p (b j n) -> p b j n", b=2, j=HJ)
        hidl = parts[:, HJ * EC * P:2 * HJ * EC * P].bitcast(BF16).rearrange("p (b j n) -> p b j n", b=2, j=HJ)

        res_dram = nc.dram_tensor("res_dram", [NTOK, C], F32, kind="Internal").ap()
        SCR = MT
        scratch = nc.dram_tensor("scratch", [SCR, JB * HEADS * N * HD], F32, kind="Internal").ap()

        x_in = [sem(f"x_in{t}") for t in range(NT)]
        tokw_in = sem("tokw_in")
        early_in = sem("early_in")
        attn_in = sem("attn_in")
        ffn_in = sem("ffn_in")
        piece_in = [sem(f"piece_in{b}") for b in range(4)]
        base_stored = [sem(f"base_stored{b}") for b in range(2)]
        o_stored = [sem(f"o_stored{i}") for i in range(2)]
        oc_loaded = [sem(f"oc_loaded{i}") for i in range(4)]
        S = {}
        for name in ("tok_psum h_ready hT_psum hT_ready e1_psum e1_ready ex_psum sq_ready nrm_ready "
                     "exn_ready rb_psum cos_ready th_ready k_psum k_ready g_psum g_ready wqg_psum wqg_ready "
                     "xs_ready hm_ready scaled xT_psum xT_ready qT_psum qv_psum qp_ready vm_ready qTm_ready r_psum rm_ready o_psum "
                     "o_ready ocT_psum ocT_ready y_psum y_read var_ready std_ready pool_chain "
                     "fb_psum fb_ready ones_ready x1_ready h1_ready x1T_psum x1T_ready x1h_ready qk_psum qk_ready v_psum v_ready vl_ready qkh_ready qkl_ready x1l_ready aol_ready vbh_ready "
                     "s_psum nmax_ready p_exp pT_psum pTh_ready pTl_ready ao_psum ao_ready aoT_psum aoT_ready pr_psum "
                     "res_ready hb_ready base_ready xn_ready xnT_psum xnT_ready "
                     "lg_psum gex_in gex_ready gts_ready gT_psum gT_ready b2_psum b2_read hid_psum hid_ready ye_psum "
                     "ye_read high_ready low_ready hidh_ready hidl_ready xnh_ready xnl_ready acc_ready res_loaded out_ready out_stored dve_chain").split():
            S[name] = sem(name)

        block = ctx.enter_context(nc.Block())
        NI = STEPS * MT

        def turn_of(q):
            return 3 + q // 2 if q < 6 else q

        def weights(q, low):
            if q < 2:
                return wqk[low][:, q].rearrange("p k c -> p (k c)"), stage[q % 4][0:HF, 0:4 * C]
            if q == 2:
                return wvp[low][:].rearrange("p a k c -> p (a k c)"), stage[q % 4][0:HF, 0:4 * C]
            e, k = (q - 3) // 3, q % 3
            if k < 2:
                return (w1h, w1l)[low][:, e, k, :], stage[q % 4][0:HF, 0:HID]
            return (w2h, w2l)[low][:, e].rearrange("p j c -> p (j c)"), stage[q % 4]

        EARLY = ["vecs", "fc1", "fc1b", "fc2", "fc2b", "ident", "sel", "rowm", "kw", "wqT", "bdm"]
        DIFF = ["wq", "wqv", "colm", "wpa", "gains"]
        FFN = ["vbb", "qkbm", "gate", "b1", "b2", "iota8"]
        tiles = dict(gains=gains, vbb=vbb, vecs=vecs, fc1=fc1, fc1b=fc1b, fc2=fc2, fc2b=fc2b, ident=ident, sel=sel, rowm=rowm,
                     kw=kw, wqT=wqT, bdm=bdm, wq=wq, wqv=wqv, colm=colm, wpa=wpa,
                     qkbm=qkbm, gate=gate, b1=b1, b2=b2, iota8=iota8)

        @block.sync
        def _(sp):
            sp.dma_start(tokw[:], d["tokw"]).then_inc(tokw_in, 16)
            for t in range(2):
                sp.dma_start(xT[:, t], d["xT"][t]).then_inc(x_in[t], 16)
            for name in EARLY:
                sp.dma_start(tiles[name][:], d[name]).then_inc(early_in, 16)
            for t in range(2, NT):
                sp.dma_start(xT[:, t], d["xT"][t]).then_inc(x_in[t], 16)
            for name in DIFF:
                sp.dma_start(tiles[name][:], d[name]).then_inc(attn_in, 16)
            for name in FFN:
                sp.dma_start(tiles[name][:], d[name]).then_inc(ffn_in, 16)
            sp.wait_ge(S["tok_psum"], NT)
            for i in range(NI + 1):
                if i < NI:
                    sp.wait_ge(S["o_ready"], i + 1)
                    for j in range(JB):
                        sp.dma_start(scratch[i % SCR].rearrange("(j h n d) -> j n h d", j=JB, h=HEADS, n=N)[j],
                                     osb[j * N:(j + 1) * N, i % 4].rearrange("p (h d) -> p h d", h=HEADS)
                                     ).then_inc(o_stored[i % 2], 16)
                if 1 <= i <= NI:
                    q = i - 1
                    sp.wait_ge(o_stored[q % 2], 16 * JB * (q // 2 + 1))
                    if q >= 4:
                        sp.wait_ge(S["ocT_psum"], q - 3)
                    sp.dma_start(oc[:, q % 4], scratch[q % SCR].rearrange("(p c) -> p c", p=T)).then_inc(oc_loaded[q % 4], 16)
                for q in range(PIECES):
                    if (turn_of(q - 4) if q >= 4 else 0) != i:
                        continue
                    if q == 2:
                        sp.wait_ge(S["e1_psum"], len(CHUNKS))
                        sp.wait_ge(S["k_psum"], 4)
                    if q >= 4:
                        sp.wait_ge(S["low_ready"], q - 3)
                    e, k = q // 3 - 1, q % 3
                    if e < 0:
                        sp.dma_start(stage[q % 4][0:HF, 0:4 * C], d["wqkvp"][q]).then_inc(piece_in[q % 4], 16)
                    elif k < 2:
                        sp.dma_start(stage[q % 4][0:HF, 0:HID], d["w1"][e, :, k]).then_inc(piece_in[q % 4], 16)
                    else:
                        sp.dma_start(stage[q % 4], d["w2"][e]).then_inc(piece_in[q % 4], 16)
            for t in range(NT):
                sp.wait_ge(S["base_ready"], t + 1)
                sp.dma_start(res_dram[t * T:(t + 1) * T], base[:, t % 2]).then_inc(base_stored[t % 2], 16)
            sp.wait_ge(base_stored[0], 16 * ((NT + 1) // 2))
            sp.wait_ge(base_stored[1], 16 * (NT // 2))
            sp.dma_start(res, res_dram[0:ET * P].rearrange("(t p) c -> p t c", p=P)).then_inc(S["res_loaded"], 16)
            out_tiles = out.rearrange("b n c -> (b n) c")
            for t in range(ET):
                sp.wait_ge(S["out_ready"], t + 1)
                sp.dma_start(out_tiles[t * P:(t + 1) * P], res[:, t]).then_inc(S["out_stored"], 16)
            sp.wait_ge(S["out_stored"], 16 * ET)

        @block.tensor
        def _(pe):
            def mm(o, l, r, start=True, stop=True):
                return nc.tensor.matmul(o, l, r, start=start, stop=stop)

            def turn(o, i):
                for f in range(2):
                    last = nc.tensor.transpose(o[:, f, :], i[:, f * HF:(f + 1) * HF], ident[0:T, 0:T])
                return last

            def halves(b):
                return bank[b][0:HF, 0:2 * T].rearrange("p (f t) -> p f t", f=2)

            halves2 = bank[0][0:HF, 2 * T:4 * T].rearrange("p (f t) -> p f t", f=2)

            def split_mm(o, left, right):
                n = len(left) * len(PASSES)
                for m, (k, (a, b)) in enumerate((k, ab) for k in range(len(left)) for ab in PASSES):
                    last = mm(o, left[k][a], right[k][b], m == 0, m == n - 1)
                return last

            pe.wait_ge(tokw_in, 16)
            for t in range(NT + 1):
                if t == 1:
                    pe.wait_ge(early_in, 16 * len(EARLY))
                if t < NT:
                    pe.wait_ge(x_in[t], 16)
                    if t >= 2:
                        pe.wait_ge(S["h_ready"], t - 1)
                    for k in range(KF):
                        last = mm(bank[t % 2][0:T, 0:C], xT[:, t, k, :], tokw[:, k, :], k == 0, k == KF - 1)
                    last.then_inc(S["tok_psum"], 1)
                if t >= 1:
                    pe.wait_ge(S["h_ready"], t)
                    if t >= 3:
                        pe.wait_ge(S["hT_ready"], t - 2)
                    turn(halves(2 + (t - 1) % 2), h[:, t - 1]).then_inc(S["hT_psum"], 1)
            for c, (t0, n) in enumerate(CHUNKS):
                pe.wait_ge(S["hT_ready"], t0 + n)
                for k in range(2):
                    last = mm(bank[4 + c][0:E1, 0:n * T], fc1[:, k, :], hT[:, k, t0 * T:(t0 + n) * T], k == 0, k == 1)
                last.then_inc(S["e1_psum"], 1)
            for i in range(4):
                t = MT - 1 + i
                for k in range(2):
                    last = mm(bank[i][0:T, 0:C], hT[:, k, t * T:(t + 1) * T], kw[:, k, :], k == 0, k == 1)
                last.then_inc(S["k_psum"], 1)
            pe.wait_ge(S["e1_ready"], len(CHUNKS))
            for t in range(NT):
                last = mm(bank[7][0:T, t * E2:(t + 1) * E2], e1T[:, t * T:(t + 1) * T], fc2[:])
            last.then_inc(S["ex_psum"], 1)
            pe.wait_ge(S["k_ready"], 4)
            for f in range(2):
                for i in range(4):
                    rows = T if i < 3 else LAST
                    a = kref[0:rows, i, f * HF:(f + 1) * HF]
                    last = mm(bank[2][0:HF, f * HF:(f + 1) * HF], a, a, i == 0, i == 3)
            last.then_inc(S["g_psum"], 1)
            pe.wait_ge(S["g_ready"], 1)
            for k in range(2):
                for f in range(2):
                    last = mm(bank[3][0:HF, k * C + f * HF:k * C + (f + 1) * HF],
                              wqT[:, f, k * HF:(k + 1) * HF], gbd[:, f, :])
            last.then_inc(S["wqg_psum"], 1)
            pe.wait_ge(S["exn_ready"], 1)
            for i in range(4):
                rows = T if i < 3 else LAST
                last = mm(bank[6][0:T, 0:E2], sel[0:rows, int(i > 0), :], ex[0:rows, MT - 1 + i, :], i == 0, i == 3)
            last.then_inc(S["rb_psum"], 1)

            pe.wait_ge(attn_in, 16 * len(DIFF))
            pe.wait_ge(S["wqg_ready"], 1)
            for i in range(NI + 5):
                q = i - 1
                if i < NI:
                    pe.wait_ge(S["xs_ready"], i + 1)
                    turn(halves(0), xs[:, i % MT]).then_inc(S["xT_psum"], 1)
                if 1 <= i <= NI:
                    pe.wait_ge(S["qp_ready"], q + 1)
                    pe.wait_ge(S["vm_ready"], q + 1)
                    if q >= 1:
                        pe.wait_ge(S["rm_ready"], q)
                    for f in range(2):
                        last = mm(bank[3 + f][0:HF, 0:JB * HF], qp[:, q % 2, f * HF:(f + 1) * HF], vm[:, q % 2, f].rearrange("p j c -> p (j c)"))
                    last.then_inc(S["r_psum"], 1)
                if i >= 5:
                    p = i - 5
                    pe.wait_ge(oc_loaded[p % 4], 16 * (p // 4 + 1))
                    turn(halves(6), oc[:, p % 4]).then_inc(S["ocT_psum"], 1)
                if i < NI:
                    pe.wait_ge(S["xT_ready"], i + 1)
                    if i >= 1:
                        pe.wait_ge(S["qTm_ready"], i)
                    for f in range(2):
                        for k in range(2):
                            last = mm(bank[1][0:HF, f * T:(f + 1) * T], wq[:, k, f * HF:(f + 1) * HF], xTs[:, i % 2, k, :], k == 0, k == 1)
                    last.then_inc(S["qT_psum"], 1)
                    for k in range(2):
                        last = mm(bank[2][0:T, 0:2 * C], xTs[:, i % 2, k, :], wqv[:, k, :], k == 0, k == 1)
                    last.then_inc(S["qv_psum"], 1)
                if 1 <= i <= NI:
                    pe.wait_ge(S["rm_ready"], q + 1)
                    pe.wait_ge(S["qTm_ready"], q + 1)
                    if q >= 1:
                        pe.wait_ge(S["o_ready"], q)
                    for f in range(2):
                        for j in range(JB):
                            last = mm(bank[5][0:T, f * HF:(f + 1) * HF], qTm[:, q % 2, f, j, :], rm[:, f, j, :], j == 0, j == JB - 1)
                    last.then_inc(S["o_psum"], 1)
                if i >= 5:
                    p = i - 5
                    pe.wait_ge(S["ocT_ready"], p + 1)
                    if p >= 1:
                        pe.wait_ge(S["y_read"], p)
                    for k in range(2):
                        last = mm(bank[7][0:T, 0:C], ocT[:, k, :], wpa[:, k, :], k == 0, k == 1)
                    last.then_inc(S["y_psum"], 1)

            values = bank[7][0:T, HEADS * (HD + 1):HEADS * (HD + 1) + C]
            def to_columns(t):
                pe.wait_ge(S["x1_ready"], t + 1)
                turn(halves(0), x1[:, t % 2]).then_inc(S["x1T_psum"], 1)

            pe.wait_ge(ffn_in, 16 * len(FFN))
            to_columns(0)
            pe.wait_ge(S["y_read"], NI)
            pe.wait_ge(S["vbh_ready"], 2)
            pe.wait_ge(S["high_ready"], PIECES)
            pe.wait_ge(S["low_ready"], PIECES)
            split_mm(bank[7][0:T, 0:C], [(vbh[:, k], vbl[:, k]) for k in range(2)],
                     [(wvp[0][:, 1, k], wvp[1][:, 1, k]) for k in range(2)]).then_inc(S["fb_psum"], 1)
            for i in range(NT + 4):
                if i < NT:
                    pe.wait_ge(S["x1h_ready"], i + 1)
                    pe.wait_ge(S["x1l_ready"], i + 1)
                    if i >= 1:
                        pe.wait_ge(S["qk_ready"], 2 * i)
                    x = [(x1Th[:, i % 2, k], x1Tl[:, i % 2, k]) for k in range(2)]
                    for a in range(2):
                        for g in range(3):
                            cols = slice(g * 128, (g + 1) * 128)
                            last = split_mm(bank[5 + a][:, g * T:(g + 1) * T], [(wqk[0][:, a, k, cols], wqk[1][:, a, k, cols]) for k in range(2)], x)
                        last.then_inc(S["qk_psum"], 1)
                if 1 <= i <= NT:
                    t = i - 1
                    for r in range(4):
                        pe.wait_ge(S["p_exp"], 4 * t + r + 1)
                        for g in range(3):
                            last = nc.tensor.transpose(bank[1 + r][0:T, g * T:(g + 1) * T], prob[:, 3 * r + g, :], ident[0:T, 0:T])
                        last.then_inc(S["pT_psum"], 1)
                if i >= 4:
                    pe.wait_ge(S["res_ready"], min(i - 3, NT))
                if i >= 5:
                    pe.wait_ge(S["xnT_ready"], i - 4)
                if i + 1 < NT:
                    to_columns(i + 1)
                if 0 <= i - 3 < NT:
                    t = i - 3
                    pe.wait_ge(S["ao_ready"], t + 1)
                    turn(halves2, ao[:, t % 2]).then_inc(S["aoT_psum"], 1)
                if 0 <= i - 2 < NT:
                    t = i - 2
                    pe.wait_ge(S["pTl_ready"], 4 * (t + 1))
                    pe.wait_ge(S["fb_ready"], 1)
                    if t >= 1:
                        pe.wait_ge(S["ao_ready"], t)
                    pe.wait_ge(S["vl_ready"], min(i, NT))
                    for hh in range(HEADS):
                        last = split_mm(bank[7][0:T, hh * (HD + 1):(hh + 1) * (HD + 1)], [(pTh[:, t % 2, hh], pTl[:, t % 2, hh])],
                                        [(v2h[:, t % 2, hh], v2l[:, t % 2, hh])])
                    last.then_inc(S["ao_psum"], 1)
                if i < NT:
                    pe.wait_ge(S["fb_ready"], 1)
                    if i >= 1:
                        pe.wait_ge(S["vl_ready"], i)
                    split_mm(values, x, [(wvp[0][:, 0, k], wvp[1][:, 0, k]) for k in range(2)]).then_inc(S["v_psum"], 1)
                if i < NT:
                    pe.wait_ge(S["qkh_ready"], 2 * (i + 1))
                    pe.wait_ge(S["qkl_ready"], 2 * (i + 1))
                    if i >= 1:
                        pe.wait_ge(S["pTl_ready"], 4 * i)
                    for g in range(3):
                        for r in range(4):
                            rows = slice(32 * r, 32 * r + 32)
                            last = split_mm(bank[1 + r][0:T, g * T:(g + 1) * T], [(qkh[rows, 0, g], qkl[rows, 0, g])],
                                            [(qkh[rows, 1, g], qkl[rows, 1, g])])
                    last.then_inc(S["s_psum"], 1)
                pe.wait_ge(S["x1T_ready"], min(i + 2, NT))
                if i >= 3:
                    pe.wait_ge(S["aol_ready"], min(i - 2, NT))
                if 0 <= i - 4 < NT:
                    t = i - 4
                    pe.wait_ge(S["xn_ready"], t + 1)
                    turn(halves2, xn[:, t % 2]).then_inc(S["xnT_psum"], 1)
                if 0 <= i - 3 < NT:
                    t = i - 3
                    pe.wait_ge(S["aoT_ready"], t + 1)
                    pe.wait_ge(S["aol_ready"], t + 1)
                    split_mm(bank[0][0:T, 0:C], [(aoTh[:, k], aoTl[:, k]) for k in range(2)],
                             [(wvp[0][:, 1, k], wvp[1][:, 1, k]) for k in range(2)]).then_inc(S["pr_psum"], 1)
            pe.wait_ge(S["xnT_ready"], NT)
            for t in range(ET):
                for k in range(2):
                    last = mm(bank[0][:, t * EXP:(t + 1) * EXP], xnT[:, k, t * P:(t + 1) * P], gate[:, k, :], k == 0, k == 1)
            last.then_inc(S["lg_psum"], 1)

            def first(i):
                e, c = i // NC, i % NC
                cols = slice(c * EC * P, (c + 1) * EC * P)
                for j in range(HJ):
                    m = i * HJ + j
                    if m >= 4:
                        pe.wait_ge(S["hid_ready"], m - 3)
                    for n, (k, (a, b)) in enumerate((k, ab) for k in range(2) for ab in PASSES):
                        last = mm(bank[2 + m % 4][:, 0:EC * P], (w1h, w1l)[a][:, e, k, j * P:(j + 1) * P], (xnh, xnl)[b][:, k, cols],
                                  n == 0, n == 5)
                    last.then_inc(S["hid_psum"], 1)

            def second(i):
                e, c = i // NC, i % NC
                pe.wait_ge(S["hidh_ready"], HJ * (i + 1))
                pe.wait_ge(S["hidl_ready"], HJ * (i + 1))
                for u in range(EC):
                    y = i * EC + u
                    if y < 2:
                        pe.wait_ge(S["acc_ready"], ET)
                    else:
                        pe.wait_ge(S["ye_read"], y - 1)
                    for n, (j, (a, b)) in enumerate((j, ab) for j in range(HJ) for ab in PASSES):
                        last = mm(bank[6 + y % 2][:, 0:C], (hidh, hidl)[a][:, i % 2, j, u * P:(u + 1) * P], (w2h, w2l)[b][:, e, j, :],
                                  n == 0, n == 3 * HJ - 1)
                    last.then_inc(S["ye_psum"], 1)

            pe.wait_ge(S["xnh_ready"], NT)
            pe.wait_ge(S["xnl_ready"], NT)
            first(0)
            pe.wait_ge(S["gts_ready"], 1)
            for t in range(ET):
                if t % 4 == 0 and t:
                    pe.wait_ge(S["gT_ready"], t // 4)
                last = nc.tensor.transpose(bank[0][0:EXP, (t % 4) * P:(t % 4 + 1) * P], gts[:, t, :], ident[:])
                if t % 4 == 3 or t == ET - 1:
                    last.then_inc(S["gT_psum"], 1)
            pe.wait_ge(S["gT_ready"], 3)
            for t in range(ET):
                if t >= 2:
                    pe.wait_ge(S["acc_ready"], t - 1)
                mm(bank[6 + t % 2][:, 0:C], gT[:, t, :], b2[:]).then_inc(S["b2_psum"], 1)
            for i in range(1, NC * EXP + 1):
                if i < NC * EXP:
                    first(i)
                second(i - 1)

        @block.scalar
        def _(act):
            def copy(o, i):
                return nc.scalar.activation(o, i, ACT.Copy)

            def halves(b):
                return bank[b][0:HF, 0:2 * T].rearrange("p (f t) -> p f t", f=2)

            halves2 = bank[0][0:HF, 2 * T:4 * T].rearrange("p (f t) -> p f t", f=2)
            for t in range(NT):
                act.wait_ge(S["hT_psum"], t + 1)
                copy(hT[:, :, t * T:(t + 1) * T], halves(2 + t % 2)).then_inc(S["hT_ready"], 1)
            for c, (t0, n) in enumerate(CHUNKS):
                act.wait_ge(S["e1_psum"], c + 1)
                nc.scalar.activation(e1T[:, t0 * T:(t0 + n) * T], bank[4 + c][0:E1, 0:n * T], ACT.Gelu, bias=fc1b[:, 0:1]).then_inc(S["e1_ready"], 1)
            for i in range(4):
                act.wait_ge(S["k_psum"], i + 1)
                src = bank[i][0:T, 0:C]
                if i == 0:
                    nc.scalar.activation(kref[:, i, :], src, ACT.Copy, scale=rowm[:, 3:4]).then_inc(S["k_ready"], 1)
                else:
                    copy(kref[:, i, :], src).then_inc(S["k_ready"], 1)
            act.wait_ge(S["sq_ready"], 1)
            nc.scalar.activation(nrm[:], nrm[:], ACT.Sqrt).then_inc(S["nrm_ready"], 1)
            act.wait_ge(S["cos_ready"], 1)
            nc.scalar.activation(th[:], cosm[:], ACT.Tanh, scale=12.5).then_inc(S["th_ready"], 1)

            def affine(o, i, which):
                for f in range(2):
                    last = nc.scalar.activation(o[:, f], i[:, f], ACT.Identity, scale=gains[:, which, 0, f:f + 1], bias=gains[:, which, 1, f:f + 1])
                return last

            for i in range(NI + 5):
                if i < NI:
                    act.wait_ge(S["xT_psum"], i + 1)
                    if i >= 2:
                        act.wait_ge(S["qv_psum"], i - 1)
                    if i < MT:
                        last = copy(xTs[:, i % 2], halves(0))
                    else:
                        last = affine(xTs[:, i % 2], halves(0), G_DIFF)
                    last.then_inc(S["xT_ready"], 1)
                if i < NT:
                    if i < MT:
                        act.wait_ge(S["xs_ready"], i + 1)
                    nc.scalar.activation(h[:, i], h[:, i], ACT.Copy, scale=mask2[:, i:i + 1] if i < MT else 2.0).then_inc(S["hm_ready"], 1)
                for q in (q for q in range(PIECES) if turn_of(q) == i):
                    act.wait_ge(piece_in[q % 4], 16 * (q // 4 + 1))
                    if q == 0:
                        act.wait_ge(S["scaled"], 1)
                    copy(*weights(q, 0)).then_inc(S["high_ready"], 1)
                if 5 <= i < NI + 5:
                    q = i - 5
                    act.wait_ge(S["ocT_psum"], q + 1)
                    if q >= 1:
                        act.wait_ge(S["y_psum"], q)
                    copy(ocT[:], halves(6)).then_inc(S["ocT_ready"], 1)
                if i == NI + 3:
                    act.wait_ge(ffn_in, 16 * len(FFN))
                    copy(vbh[:], vbb[:]).then_inc(S["vbh_ready"], 1)
                if i < NI:
                    act.wait_ge(S["qv_psum"], i + 1)
                    if i >= 2:
                        act.wait_ge(S["r_psum"], i - 1)
                    copy(qp[:, i % 2], bank[2][0:T, 0:C]).then_inc(S["qp_ready"], 1)
                    for j in range(JB):
                        last = nc.scalar.activation(vm[:, i % 2, :, j, :], bank[2][0:T, C:2 * C].rearrange("p (f c) -> p f c", f=2), ACT.Copy, scale=rowm[:, j:j + 1])
                    last.then_inc(S["vm_ready"], 1)
                if 1 <= i <= NI:
                    q = i - 1
                    act.wait_ge(S["o_psum"], q + 1)
                    if q >= 4:
                        act.wait_ge(oc_loaded[q % 4], 16 * (q // 4))
                    copy(osb[:, q % 4], bank[5][0:T, 0:C]).then_inc(S["o_ready"], 1)

            act.wait_ge(S["low_ready"], PIECES)

            def columns(t):
                act.wait_ge(S["x1T_psum"], t + 1)
                if t >= 1:
                    act.wait_ge(S["x1l_ready"], t)
                affine(x1T, halves(0), G_LN1).then_inc(S["x1T_ready"], 1)
                act.wait_ge(S["x1T_ready"], t + 1)
                if t >= 2:
                    act.wait_ge(S["v_psum"], t - 1)
                copy(x1Th[:, t % 2], x1T).then_inc(S["x1h_ready"], 1)

            values = bank[7][0:T, HEADS * (HD + 1):HEADS * (HD + 1) + C]
            columns(0)
            act.wait_ge(S["ones_ready"], 1)
            for i in range(NT + 5):
                if 1 <= i <= NT:
                    t = i - 1
                    if t >= 1:
                        act.wait_ge(S["pT_psum"], 4 * t)
                    for r in range(4):
                        act.wait_ge(S["nmax_ready"], 4 * t + r + 1)
                        for g in range(3):
                            hh = 3 * r + g
                            last = nc.scalar.activation(prob[:, hh, :], bank[1 + r][0:T, g * T:(g + 1) * T], ACT.Exp,
                                                        bias=nmax[:, hh:hh + 1])
                        last.then_inc(S["p_exp"], 1)
                if 0 <= i - 5 < NT:
                    t = i - 5
                    act.wait_ge(S["xnT_psum"], t + 1)
                    act.wait_ge(S["res_ready"], min(t + 2, NT))
                    affine(xnT[:, :, t * T:(t + 1) * T], halves2, G_LN2).then_inc(S["xnT_ready"], 1)
                if i < NT:
                    for a in range(2):
                        act.wait_ge(S["qk_ready"], 2 * i + a + 1)
                        if i >= 1 and a == 0:
                            act.wait_ge(S["s_psum"], i)
                        copy(qkh[:, a], qkT[:, a]).then_inc(S["qkh_ready"], 1)
                if 1 <= i <= NT:
                    t = i - 1
                    if t >= 2:
                        act.wait_ge(S["ao_psum"], t - 1)
                    for r in range(4):
                        act.wait_ge(S["pT_psum"], 4 * t + r + 1)
                        copy(pTh[:, t % 2, 3 * r:3 * r + 3, :].rearrange("p a b -> p (a b)"), bank[1 + r][0:T, 0:3 * T]).then_inc(S["pTh_ready"], 1)
                if 0 <= i - 3 < NT:
                    act.wait_ge(S["aoT_psum"], i - 2)
                    if i >= 4:
                        act.wait_ge(S["pr_psum"], i - 3)
                    copy(aoTh, halves2).then_inc(S["aoT_ready"], 1)
                if i + 1 < NT:
                    columns(i + 1)
                if i < NT:
                    act.wait_ge(S["v_psum"], i + 1)
                    if i >= 2:
                        act.wait_ge(S["ao_ready"], i - 1)
                    copy(v2h[:, i % 2, :, 0:HD], values.rearrange("p (u d) -> p u d", u=HEADS)).then_inc(S["v_ready"], 1)

            def hidden(i0, i1):
                for i in range(i0, i1):
                    e = i // NC
                    for j in range(HJ):
                        m = i * HJ + j
                        act.wait_ge(S["hid_psum"], m + 1)
                        if m >= NH:
                            act.wait_ge(S["hidl_ready"], m - NH + 1)
                        nc.scalar.activation(hidf[:, m % NH], bank[2 + m % 4][:, 0:EC * P], ACT.Gelu, bias=b1[:, e, j:j + 1]).then_inc(S["hid_ready"], 1)

            act.wait_ge(S["gex_in"], 1)
            nc.scalar.activation(vv[:, 3, :], vv[:, 2, :], ACT.Exp).then_inc(S["gex_ready"], 1)
            hidden(0, 1)
            for c in range(3):
                act.wait_ge(S["gT_psum"], c + 1)
                n = min(4, ET - 4 * c)
                copy(gT[:, 4 * c:4 * c + n, :].rearrange("p a b -> p (a b)"), bank[0][0:EXP, 0:n * P]).then_inc(S["gT_ready"], 1)
            hidden(1, NC * EXP)

        @block.vector
        def _(dve):
            V = nc.vector
            halves2 = bank[0][0:HF, 2 * T:4 * T].rearrange("p (f t) -> p f t", f=2)
            chain = [0]
            n_ln = [0]

            def link(ins):
                chain[0] += 1
                ins.then_inc(S["dve_chain"], 1)
                dve.wait_ge(S["dve_chain"], chain[0])

            def vec(v):
                return vecs[:, v, :]

            def moments(x):
                b = n_ln[0] % 2
                if n_ln[0] >= 2:
                    dve.wait_ge(S["var_ready"], n_ln[0] - 1)
                link(V.bn_stats(stats[0:x.shape[0], b], x))
                n_ln[0] += 1
                V.bn_aggr(mv[0:x.shape[0], (n_ln[0] - 1) % 4], stats[0:x.shape[0], b]).then_inc(S["var_ready"], 1)
                return n_ln[0] - 1

            def centred(o, x, n, r=rstd):
                rows = x.shape[0]
                return V.tensor_scalar(o, x, mv[0:rows, n % 4, 0:1], r[0:rows, n % 4:n % 4 + 1], ALU.subtract, ALU.mult)

            dve.wait_ge(early_in, 16 * len(EARLY))
            for t in range(NT):
                dve.wait_ge(S["tok_psum"], t + 1)
                V.tensor_tensor(h[:, t], bank[t % 2][0:T, 0:C], vec(V_TOKB), ALU.add).then_inc(S["h_ready"], 1)
            dve.wait_ge(S["ex_psum"], 1)
            link(V.tensor_tensor(ex[:], bank[7][0:T, 0:NT * E2].rearrange("p (t e) -> p t e", t=NT),
                                 fc2b[:, None, :].broadcast_to([T, NT, E2]), ALU.add))
            link(V.tensor_tensor(exs[:], ex[:], ex[:], ALU.mult))
            V.tensor_reduce(nrm[:], exs[:], AX_X, ALU.add).then_inc(S["sq_ready"], 1)
            dve.wait_ge(S["g_psum"], 1)
            V.tensor_tensor(gbd[:], bank[2][0:HF, 0:C].rearrange("p (f c) -> p f c", f=2),
                            bdm[:, 1:2, :].broadcast_to([HF, 2, HF]), ALU.mult).then_inc(S["g_ready"], 1)
            dve.wait_ge(S["wqg_psum"], 1)
            dve.wait_ge(attn_in, 16 * len(DIFF))
            V.tensor_copy(wqv[:, :, 0:C], bank[3][0:HF, 0:2 * C].rearrange("p (k c) -> p k c", k=2)).then_inc(S["wqg_ready"], 1)
            dve.wait_ge(S["nrm_ready"], 1)
            link(V.tensor_scalar(nrm[:], nrm[:], COS_EPS, None, ALU.max))
            link(V.reciprocal(nrm[:], nrm[:]))
            V.tensor_tensor(ex[:], ex[:], nrm[:, :, None].broadcast_to([T, NT, E2]), ALU.mult).then_inc(S["exn_ready"], 1)
            dve.wait_ge(S["rb_psum"], 1)
            dve.wait_ge(S["exn_ready"], 1)
            link(V.tensor_copy(rb[:], bank[6][0:T, 0:E2]))
            link(V.tensor_tensor(exs[:, 0:MT], ex[:, 0:MT], rb[:, None, :].broadcast_to([T, MT, E2]), ALU.mult))
            V.tensor_reduce(cosm[:], exs[:, 0:MT], AX_X, ALU.add).then_inc(S["cos_ready"], 1)
            dve.wait_ge(S["th_ready"], 1)
            link(V.tensor_scalar(mask[:], th[:], 0.5, 0.5, ALU.mult, ALU.add))
            link(V.tensor_tensor(mask[:, MT - 1:MT], mask[:, MT - 1:MT], rowm[:, 0:1], ALU.mult))
            link(V.tensor_scalar(mask2[:], mask[:], -1.0, 2.0, ALU.mult, ALU.add))
            for t in range(MT):
                V.tensor_scalar(xs[:, t], h[:, t], mask[:, t:t + 1], None, ALU.mult).then_inc(S["xs_ready"], 1)

            first = {}

            def combine(t):
                dve.wait_ge(S["hm_ready"], t + 1)
                if t < MT:
                    link(V.scalar_tensor_tensor(out=xs[:, t], in0=xs[:, t], scalar=mask[:, t:t + 1], in1=h[:, t], op0=ALU.mult, op1=ALU.add))
                first[t] = moments((xs if t < MT else h)[:, t])

            def normalise(t):
                dve.wait_ge(S["std_ready"], first[t] + 1)
                if t >= 2:
                    dve.wait_ge(S["x1T_psum"], t - 1)
                src = (xs if t < MT else h)[:, t]
                centred(x1[:, t % 2], src, first[t], rstd1).then_inc(S["x1_ready"], 1)
                centred(h1[:, t], src, first[t]).then_inc(S["h1_ready"], 1)

            turned = {}
            for i in range(NI + 6):
                if 1 <= i <= NI:
                    q = i - 1
                    dve.wait_ge(S["r_psum"], q + 1)
                    if q >= 1:
                        dve.wait_ge(S["o_psum"], q)
                    for f in range(2):
                        last = V.tensor_tensor(rm[:, f], bank[3 + f][0:HF, 0:JB * HF].rearrange("p (j c) -> p j c", j=JB),
                                               bdm[:, 0:1, :].broadcast_to([HF, JB, HF]), ALU.mult)
                    last.then_inc(S["rm_ready"], 1)
                if i < NI:
                    dve.wait_ge(S["qT_psum"], i + 1)
                    if i >= 2:
                        dve.wait_ge(S["o_psum"], i - 1)
                    for f in range(2):
                        last = V.tensor_tensor(qTm[:, i % 2, f], bank[1][0:HF, f * T:(f + 1) * T][:, None, :].broadcast_to([HF, JB, T]), colm[:], ALU.mult)
                    last.then_inc(S["qTm_ready"], 1)
                if i == 2:
                    dve.wait_ge(piece_in[0], 16)
                    V.tensor_scalar(stage[0][0:HF, 0:4 * C], stage[0][0:HF, 0:4 * C], SCALE, None, ALU.mult).then_inc(S["scaled"], 1)
                if 5 <= i < NI + 5:
                    q = i - 5
                    dve.wait_ge(S["y_psum"], q + 1)
                    V.tensor_tensor(yb[:, q % 2], bank[7][0:T, 0:C], vec(V_APB), ALU.add).then_inc(S["y_read"], 1)
                    dve.wait_ge(S["y_read"], q + 1)
                    turned[q] = moments(yb[:, q % 2])
                if i >= 6:
                    q = i - 6
                    dve.wait_ge(S["std_ready"], turned[q] + 1)
                    dve.wait_ge(S["xT_psum"], q + 1)
                    if q < NI - MT:
                        centred(xs[:, q % MT], yb[:, q % 2], turned[q]).then_inc(S["xs_ready"], 1)
                    else:
                        link(centred(xs[:, q % MT], yb[:, q % 2], turned[q]))
                        link(V.tensor_tensor(xs[:, q % MT], xs[:, q % MT], vec(V_ALG), ALU.mult))
                        link(V.tensor_tensor(xs[:, q % MT], xs[:, q % MT], vec(V_ALB), ALU.add))
                if i == NI + 3:
                    dve.wait_ge(S["vbh_ready"], 1)
                    V.tensor_tensor(vbl[:], vbb[:], vbh[:], ALU.subtract).then_inc(S["vbh_ready"], 1)
                if NI + 1 <= i <= NI + 3:
                    combine(i - NI - 1)
                if NI + 2 <= i <= NI + 3:
                    normalise(i - NI - 2)
                if i == NI + 4:
                    link(V.memset(v2l[:, :, :, HD:HD + 1], 0.0))
                    V.memset(v2h[:, :, :, HD:HD + 1], 1.0).then_inc(S["ones_ready"], 1)
            dve.wait_ge(S["low_ready"], PIECES)
            def columns_low(t):
                dve.wait_ge(S["x1h_ready"], t + 1)
                V.tensor_tensor(x1Tl[:, t % 2], x1T, x1Th[:, t % 2], ALU.subtract).then_inc(S["x1l_ready"], 1)

            columns_low(0)
            dve.wait_ge(S["fb_psum"], 1)
            V.tensor_tensor(fbias[:], bank[7][0:T, 0:C], vec(V_FPB), ALU.add).then_inc(S["fb_ready"], 1)
            dve.wait_ge(ffn_in, 16 * len(FFN))
            link(V.tensor_scalar(qkbm[:, 0], qkbm[:, 0], SCALE, None, ALU.mult))

            def high(t):
                cols = slice(t * T, (t + 1) * T)
                dve.wait_ge(S["xnT_ready"], t + 1)
                V.tensor_copy(xnh[:, :, cols], xnT[:, :, cols]).then_inc(S["xnh_ready"], 1)

            values = bank[7][0:T, HEADS * (HD + 1):HEADS * (HD + 1) + C]
            for i in range(NT + 5):
                if 1 <= i <= NT:
                    t = i - 1
                    dve.wait_ge(S["s_psum"], t + 1)
                    for r in range(4):
                        hs = slice(3 * r, 3 * r + 3)
                        V.tensor_reduce(nmax[:, hs], bank[1 + r][0:T, 0:3 * T].rearrange("p (u m) -> p u m", u=3), AX_X, ALU.max, negate=True).then_inc(S["nmax_ready"], 1)
                if 0 <= i - 4 < NT:
                    t = i - 4
                    dve.wait_ge(S["pr_psum"], t + 1)
                    dve.wait_ge(S["hb_ready"], t + 1)
                    if t >= 2:
                        dve.wait_ge(S["base_ready"], t - 1)
                    V.tensor_tensor(yb[:, t % 2], bank[0][0:T, 0:C], hb[:, t % 2], ALU.add).then_inc(S["res_ready"], 1)
                if i < NT:
                    for a in range(2):
                        dve.wait_ge(S["qk_psum"], 2 * i + a + 1)
                        if i >= 1 and a == 0:
                            dve.wait_ge(S["qkh_ready"], 2 * i)
                            dve.wait_ge(S["qkl_ready"], 2 * i)
                        V.tensor_tensor(qkT[:, a].rearrange("p g t -> p (g t)"), bank[5 + a][:, 0:3 * T],
                                        qkbm[:, a].rearrange("p g t -> p (g t)"), ALU.add).then_inc(S["qk_ready"], 1)
                second = None
                if 0 <= i - 4 < NT:
                    t = i - 4
                    dve.wait_ge(S["res_ready"], t + 1)
                    second = moments(yb[:, t % 2])
                if i + 2 < NT:
                    normalise(i + 2)
                if i + 3 < NT:
                    combine(i + 3)
                if second is not None:
                    dve.wait_ge(S["std_ready"], second + 1)
                    if t >= 2:
                        dve.wait_ge(S["xnT_psum"], t - 1)
                    centred(xn[:, t % 2], yb[:, t % 2], second).then_inc(S["xn_ready"], 1)
                if 1 <= i <= NT:
                    t = i - 1
                    for r in range(4):
                        dve.wait_ge(S["pTh_ready"], 4 * t + r + 1)
                        hs = slice(3 * r, 3 * r + 3)
                        V.tensor_tensor(pTl[:, t % 2, hs].rearrange("p a b -> p (a b)"), bank[1 + r][0:T, 0:3 * T],
                                        pTh[:, t % 2, hs].rearrange("p a b -> p (a b)"), ALU.subtract).then_inc(S["pTl_ready"], 1)
                if 0 <= i - 2 < NT:
                    t = i - 2
                    dve.wait_ge(S["ao_psum"], t + 1)
                    dve.wait_ge(S["v_psum"], min(i + 1, NT))
                    if t >= 2:
                        dve.wait_ge(S["aoT_psum"], t - 1)
                    heads = bank[7][0:T, 0:HEADS * (HD + 1)].rearrange("p (u d) -> p u d", u=HEADS)
                    link(V.reciprocal(prec[:], heads[:, :, HD]))
                    V.tensor_tensor(ao[:, t % 2].rearrange("p (u d) -> p u d", u=HEADS), heads[:, :, 0:HD],
                                    prec[:, :, None].broadcast_to([T, HEADS, HD]), ALU.mult).then_inc(S["ao_ready"], 1)
                if 0 <= i - 3 < NT:
                    t = i - 3
                    dve.wait_ge(S["aoT_ready"], t + 1)
                    dve.wait_ge(S["x1T_ready"], min(i + 2, NT))
                    V.tensor_tensor(aoTl, halves2, aoTh, ALU.subtract).then_inc(S["aol_ready"], 1)
                if i + 1 < NT:
                    columns_low(i + 1)
                if i < NT:
                    dve.wait_ge(S["v_ready"], i + 1)
                    V.tensor_tensor(v2l[:, i % 2, :, 0:HD], values.rearrange("p (u d) -> p u d", u=HEADS),
                                    v2h[:, i % 2, :, 0:HD], ALU.subtract).then_inc(S["vl_ready"], 1)
                if 0 <= i - 5 < NT:
                    high(i - 5)

            dve.wait_ge(S["lg_psum"], 1)
            link(V.tensor_copy(lg[:], bank[0][:, 0:ET * EXP].rearrange("p (t e) -> p t e", t=ET)))

            def wide(v):
                return v[:, :, None].broadcast_to([P, ET, EXP])

            def rows8(k):
                return iota8[:, k:k + 1, :].broadcast_to([P, ET, EXP])

            for n, m in ((0, m1), (1, m2)):
                link(V.tensor_reduce(vv[:, n, :], lg[:], AX_X, ALU.max))
                link(V.tensor_tensor(m[:], lg[:], wide(vv[:, n, :]), ALU.is_equal))
                link(V.tensor_tensor(lt[:], m[:], rows8(1), ALU.mult))
                link(V.tensor_reduce(vv[:, 4, :], lt[:], AX_X, ALU.min))
                link(V.tensor_tensor(m[:], rows8(1), wide(vv[:, 4, :]), ALU.is_equal))
                if n == 0:
                    link(V.tensor_scalar(lt[:], m[:], -3.0e38, None, ALU.mult))
                    link(V.scalar_tensor_tensor(out=lg[:], in0=lt[:], scalar=0.0, in1=lg[:], op0=ALU.add, op1=ALU.add))
            V.tensor_tensor(vv[:, 2, :], vv[:, 1, :], vv[:, 0, :], ALU.subtract).then_inc(S["gex_in"], 1)
            dve.wait_ge(S["gex_ready"], 1)
            link(V.tensor_scalar(vv[:, 4, :], vv[:, 3, :], 1.0, None, ALU.add))
            link(V.reciprocal(vv[:, 4, :], vv[:, 4, :]))
            link(V.tensor_tensor(vv[:, 5, :], vv[:, 3, :], vv[:, 4, :], ALU.mult))
            link(V.tensor_tensor(m1[:], m1[:], wide(vv[:, 4, :]), ALU.mult))
            link(V.tensor_tensor(m2[:], m2[:], wide(vv[:, 5, :]), ALU.mult))
            V.tensor_tensor(gts[:], m1[:], m2[:], ALU.add).then_inc(S["gts_ready"], 1)
            dve.wait_ge(S["gts_ready"], 1)
            def split(i):
                for j in range(HJ):
                    m = i * HJ + j
                    dve.wait_ge(S["hid_ready"], m + 1)
                    if i >= 2 and j == 0:
                        dve.wait_ge(S["ye_psum"], EC * (i - 1))
                    V.tensor_copy(hidh[:, i % 2, j], hidf[:, m % NH]).then_inc(S["hidh_ready"], 1)
                    dve.wait_ge(S["hidh_ready"], m + 1)
                    V.tensor_tensor(hidl[:, i % 2, j], hidf[:, m % NH], hidh[:, i % 2, j], ALU.subtract).then_inc(S["hidl_ready"], 1)

            split(0)
            for t in range(ET):
                dve.wait_ge(S["b2_psum"], t + 1)
                V.tensor_copy(acc[:, t], bank[6 + t % 2][:, 0:C]).then_inc(S["acc_ready"], 1)
            dve.wait_ge(S["acc_ready"], ET)
            for i in range(1, NC * EXP + 1):
                if i < NC * EXP:
                    split(i)
                e, c = (i - 1) // NC, (i - 1) % NC
                for u in range(EC):
                    y, t = (i - 1) * EC + u, c * EC + u
                    dve.wait_ge(S["ye_psum"], y + 1)
                    if e:
                        dve.wait_ge(S["ye_read"], y - ET + 1)
                    V.scalar_tensor_tensor(out=acc[:, t], in0=bank[6 + y % 2][:, 0:C], scalar=gts[:, t, e:e + 1], in1=acc[:, t],
                                           op0=ALU.mult, op1=ALU.add).then_inc(S["ye_read"], 1)
            dve.wait_ge(S["res_loaded"], 16)
            last_n = {}
            for t in range(ET + 1):
                if t < ET:
                    dve.wait_ge(S["ye_read"], EC * NC * (EXP - 1) + t + 1)
                    link(V.tensor_tensor(acc[:, t], acc[:, t], res[:, t], ALU.add))
                    last_n[t] = moments(acc[:, t])
                if t >= 1:
                    n = last_n[t - 1]
                    dve.wait_ge(S["std_ready"], n + 1)
                    centred(res[:, t - 1], acc[:, t - 1], n).then_inc(S["out_ready"], 1)

        @block.gpsimd
        def _(pool):
            G = nc.gpsimd
            chain, n_ln = [0], [0]

            def link(ins):
                chain[0] += 1
                ins.then_inc(S["pool_chain"], 1)
                pool.wait_ge(S["pool_chain"], chain[0])

            def root(twice=False, rows=T):
                n = n_ln[0]
                k = slice(n % 4, n % 4 + 1)
                n_ln[0] += 1
                var = mv[0:rows, n % 4, 1:2]
                pool.wait_ge(S["var_ready"], n + 1)
                ve = veps[0:rows]
                link(G.tensor_scalar(ve, var, EPS, None, ALU.add))
                last = G.tensor_tensor(rstd[0:rows, k], ve, nhalf[0:rows], ALU.pow)
                if twice:
                    link(last)
                    link(G.tensor_tensor(ve, var, rstd[0:rows, k], ALU.mult))
                    link(G.tensor_tensor(ve, ve, rstd[0:rows, k], ALU.mult))
                    link(G.tensor_scalar(ve, ve, EPS, None, ALU.add))
                    link(G.tensor_tensor(ve, ve, nhalf[0:rows], ALU.pow))
                    last = G.tensor_tensor(rstd1[:, k], ve, rstd[0:rows, k], ALU.mult)
                last.then_inc(S["std_ready"], 1)
                pool.wait_ge(S["std_ready"], n + 1)

            link(G.memset(nhalf[:], -0.5))
            for i in range(3, NI + 6):
                if 5 <= i < NI + 5:
                    root()
                if NI + 1 <= i <= NI + 3:
                    root(twice=True)
                for q in (q for q in range(PIECES) if turn_of(q) == i):
                    o, w = weights(q, 1)
                    pool.wait_ge(S["high_ready"], q + 1)
                    G.tensor_tensor(o, w, weights(q, 0)[0], ALU.subtract).then_inc(S["low_ready"], 1)
            def low(t):
                cols = slice(t * T, (t + 1) * T)
                pool.wait_ge(S["xnh_ready"], t + 1)
                G.tensor_tensor(xnl[:, :, cols], xnT[:, :, cols], xnh[:, :, cols], ALU.subtract).then_inc(S["xnl_ready"], 1)

            for i in range(NT + 5):
                if 0 <= i - 4 < NT:
                    root()
                if i < NT:
                    for a in range(2):
                        pool.wait_ge(S["qkh_ready"], 2 * i + a + 1)
                        if i >= 1 and a == 0:
                            pool.wait_ge(S["s_psum"], i)
                        G.tensor_tensor(qkl[:, a], qkT[:, a], qkh[:, a], ALU.subtract).then_inc(S["qkl_ready"], 1)
                if i + 3 < NT:
                    root(twice=True)
                if 0 <= i - 4 < NT:
                    t = i - 4
                    pool.wait_ge(S["res_ready"], t + 1)
                    if t >= 2:
                        pool.wait_ge(base_stored[t % 2], 16 * (t // 2))
                    G.tensor_tensor(base[:, t % 2], yb[:, t % 2], h1[:, t], ALU.add).then_inc(S["base_ready"], 1)
                if 0 <= i - 3 < NT:
                    t = i - 3
                    pool.wait_ge(S["h1_ready"], t + 1)
                    pool.wait_ge(S["fb_ready"], 1)
                    if t >= 2:
                        pool.wait_ge(S["res_ready"], t - 1)
                    G.tensor_tensor(hb[:, t % 2], h1[:, t], fbias[:], ALU.add).then_inc(S["hb_ready"], 1)
                if 0 <= i - 5 < NT:
                    low(i - 5)
            for t in range(ET):
                root(rows=P)

def kernel(**inputs):
    import numpy as np
    import concourse.bacc as bacc
    from concourse.bass_utils import run_bass_kernel_spmd

    a = {k.replace("L0_", ""): np.asarray(v) for k, v in inputs.items()}

    def halves(w):
        return w.reshape(2, HF, -1).transpose(1, 0, 2)

    x = np.zeros((NT * JB, N, KF * 128), np.float32)
    x[:B] = a["x"].reshape(B, 3, 6, 16, 6, 16).transpose(0, 2, 4, 1, 3, 5).reshape(B, N, -1)
    image = np.arange(T) // N
    place = np.arange(T) % N
    head = np.arange(HF) // HD
    same = (place[:, None] == place[None, :]) * np.float32(1.0 / NREF)
    sel = np.stack([same * (np.arange(T) >= FIRST_REF)[:, None], same], 1)
    qkv_w, qkv_b = a["ffn_qkv_w"], a["ffn_qkv_b"]
    wqkp = np.zeros((C, 2, HEADS, 32), np.float32)
    order = np.arange(HEADS).reshape(4, 3).T.reshape(-1)
    wqkp[:, :, :, :HD] = qkv_w[:, :2 * C].reshape(C, 2, HEADS, HD)[:, :, order]
    qkbm = np.zeros((2, 3, 4, 32, T), np.float32)
    qkbm[:, :, :, :HD] = qkv_b[:2 * C].reshape(2, HEADS, HD)[:, order].reshape(2, 3, 4, HD)[..., None]
    for j in range(JB):
        for u in range(5):
            qkbm[0, :, :, HD + 3 * u + j] = np.where(image != j, np.float32(BAR), np.float32(0))
            qkbm[1, :, :, HD + 3 * u + j] = np.where(image == j, np.float32(-BAR), np.float32(0))
    vec = [a["tok_b"], a["attn_proj_b"], a["attn_ln_g"], a["attn_ln_b"], a["ffn_proj_b"]]
    gains = [[a[ln + "_g"], a[ln + "_b"]] for ln in ("attn_ln", "ffn_ln1", "ffn_ln2")]
    e = np.arange(EXP)
    data = {
        "xT": x.reshape(NT, T, KF, 128).transpose(0, 3, 2, 1),
        "tokw": a["tok_W"].reshape(C, KF, 128).transpose(2, 1, 0),
        "vecs": np.broadcast_to(np.stack(vec)[None], (T, 5, C)),
        "gains": np.stack([np.stack(g) for g in gains]).reshape(3, 2, 2, HF).transpose(3, 0, 1, 2),
        "vbb": np.broadcast_to(halves(qkv_b[2 * C:, None]), (HF, 2, T)),
        "fc1": halves(a["attn_fc1_w"]), "fc1b": a["attn_fc1_b"][:, None], "fc2": a["attn_fc2_w"],
        "fc2b": np.broadcast_to(a["attn_fc2_b"][None], (T, E2)),
        "kw": halves(a["attn_k_w"]), "wqv": halves(a["attn_qv_w"]),
        "wq": halves(a["attn_qv_w"][:, :C]), "wqT": halves(a["attn_qv_w"][:, :C].T),
        "wpa": halves(a["attn_proj_w"]),
        "wqkvp": np.stack([halves(wqkp[:, 0]).reshape(HF, -1), halves(wqkp[:, 1]).reshape(HF, -1),
                           np.stack([halves(qkv_w[:, 2 * C:]), halves(a["ffn_proj_w"])], 1).reshape(HF, -1)]),
        "qkbm": qkbm.reshape(2, 3, 128, T).transpose(2, 0, 1, 3),
        "gate": halves(a["ffn_gate_w"]),
        "w1": a["ffn_w1"].reshape(EXP, 2, HF, HID).transpose(0, 2, 1, 3),
        "w2": a["ffn_w2"].reshape(EXP, HJ, 128, C).transpose(0, 2, 1, 3),
        "b1": a["ffn_b1"].reshape(EXP, HJ, 128).transpose(2, 0, 1), "b2": a["ffn_b2"],
        "ident": np.eye(P), "sel": sel,
        "colm": np.broadcast_to((image[None] == np.arange(JB)[:, None])[None], (HF, JB, T)),
        "rowm": np.stack([image == 0, image == 1, image == 2, np.arange(T) >= FIRST_REF], 1),
        "bdm": np.stack([(head[:, None] == head[None]) * 1.0, (head[:, None] == head[None]) / (HD * NREF)], 1),
        "iota8": np.broadcast_to(np.stack([e, e - EXP])[None], (P, 2, EXP)),
    }
    nc = bacc.Bacc("TRN2", target_bir_lowering=False, num_devices=1)
    arrays, aps = {}, {}
    for name, v in data.items():
        v = np.ascontiguousarray(v, dtype=np.float32)
        arrays["in_" + name] = v
        aps[name] = nc.dram_tensor("in_" + name, v.shape, F32, kind="ExternalInput").ap()
    out = nc.dram_tensor("out", (B, N, C), F32, kind="ExternalOutput").ap()
    vit_kernel(nc, aps, out)
    r = run_bass_kernel_spmd(nc, [arrays], core_ids=[0])
    return r.results[0]["out"]
```
